# Optimizing a Trainium2 kernel written in Bass

```python
import numpy as np
import jax
import jax.numpy as jnp

def _softmax(x, axis=-1):
    return jax.nn.softmax(x, axis=axis)

def _gelu(x):
    return jax.nn.gelu(x, approximate=True)

def _silu(x):
    return jax.nn.silu(x)

def _sigmoid(x):
    return jax.nn.sigmoid(x)

def _layernorm(x, axis=-1, eps=1e-05):
    m = jnp.mean(x, axis=axis, keepdims=True)
    v = jnp.var(x, axis=axis, keepdims=True)
    return (x - m) / jnp.sqrt(v + eps)

def _scatter_add(tgt, idx, src, axis=0):
    return tgt.at[idx].add(src)

def _segment_sum(src, seg, n):
    return jax.ops.segment_sum(src, seg, n)
kernel_name = 'mk_seq_postln_d1_jaxref_r8_754dcf'

def setup_inputs(seed: int=0):
    np.random.seed(seed)
    _w = jnp.asarray

    def _L0_attn_setup():
        import jax, jax.numpy as jnp
        import numpy as np
        D_MODEL, STATE, N_EXP, VOCAB = (128, 16, 4, 4000)
        B, L = (4, 256)
        EPS = 1e-05
        key = jax.random.key(seed)
        ks = jax.random.split(key, 20)
        d, s, e, f = (D_MODEL, STATE, N_EXP, 4 * D_MODEL)
        sc = 0.02
        inp = {'x': jax.random.normal(ks[0], (B, L, d), jnp.float32), 'A_log': jnp.log(jax.random.uniform(ks[1], (d, s)) * 0.9 + 0.1), 'D_param': jnp.ones((d,), jnp.float32), 'Wd': jax.random.normal(ks[2], (d, d)) * sc, 'bd': jnp.zeros((d,)), 'WB': jax.random.normal(ks[3], (d, s)) * sc, 'bB': jnp.zeros((s,)), 'WC': jax.random.normal(ks[4], (d, s)) * sc, 'bC': jnp.zeros((s,)), 'Wr': jax.random.normal(ks[5], (d, e)) * sc, 'br': jnp.zeros((e,)), 'up_w': jax.random.normal(ks[6], (e, d, f)) * sc, 'up_b': jnp.zeros((e, f)), 'down_w': jax.random.normal(ks[7], (e, f, d)) * sc, 'down_b': jnp.zeros((e, d)), 'ln_w': jnp.ones((d,)), 'ln_b': jnp.zeros((d,))}
        return inp
    _L0_attn_in = _L0_attn_setup()

    def _L0_ffn_setup():
        import jax, jax.numpy as jnp
        import numpy as np
        DIM = 128
        HIDDEN = 384
        SCALE = 1.0 / 127.0

        def _dequant(w_int, dtype):
            return w_int.astype(dtype) * jnp.asarray(SCALE, dtype)
        key = jax.random.key(seed)
        k_x, k_g, k_u, k_d = jax.random.split(key, 4)
        x = jax.random.normal(k_x, (4, 256, DIM), dtype=jnp.float32)
        w_gate = jax.random.randint(k_g, (HIDDEN, DIM), -127, 128, dtype=jnp.int32)
        w_up = jax.random.randint(k_u, (HIDDEN, DIM), -127, 128, dtype=jnp.int32)
        w_down = jax.random.randint(k_d, (DIM, HIDDEN), -127, 128, dtype=jnp.int32)
        return {'x': x, 'w_gate': w_gate, 'w_up': w_up, 'w_down': w_down}
    _L0_ffn_in = _L0_ffn_setup()
    _d = {'L0_attn_x': _L0_attn_in['x'], 'L0_attn_A_log': _L0_attn_in['A_log'], 'L0_attn_D_param': _L0_attn_in['D_param'], 'L0_attn_Wd': _L0_attn_in['Wd'], 'L0_attn_bd': _L0_attn_in['bd'], 'L0_attn_WB': _L0_attn_in['WB'], 'L0_attn_bB': _L0_attn_in['bB'], 'L0_attn_WC': _L0_attn_in['WC'], 'L0_attn_bC': _L0_attn_in['bC'], 'L0_attn_Wr': _L0_attn_in['Wr'], 'L0_attn_br': _L0_attn_in['br'], 'L0_attn_up_w': _L0_attn_in['up_w'], 'L0_attn_up_b': _L0_attn_in['up_b'], 'L0_attn_down_w': _L0_attn_in['down_w'], 'L0_attn_down_b': _L0_attn_in['down_b'], 'L0_attn_ln_w': _L0_attn_in['ln_w'], 'L0_attn_ln_b': _L0_attn_in['ln_b'], 'L0_ffn_w_gate': _L0_ffn_in['w_gate'], 'L0_ffn_w_up': _L0_ffn_in['w_up'], 'L0_ffn_w_down': _L0_ffn_in['w_down']}
    _x0 = _d['L0_attn_x']
    _d['L0_attn_x'] = jax.random.normal(jax.random.fold_in(jax.random.key(seed), 1), (8, 1024, 128), dtype=_x0.dtype)
    del _x0
    return _d

def reference(L0_attn_x, L0_attn_A_log, L0_attn_D_param, L0_attn_Wd, L0_attn_bd, L0_attn_WB, L0_attn_bB, L0_attn_WC, L0_attn_bC, L0_attn_Wr, L0_attn_br, L0_attn_up_w, L0_attn_up_b, L0_attn_down_w, L0_attn_down_b, L0_attn_ln_w, L0_attn_ln_b, L0_ffn_w_gate, L0_ffn_w_up, L0_ffn_w_down):

    def _L0_attn_ref(x, A_log, D_param, Wd, bd, WB, bB, WC, bC, Wr, br, up_w, up_b, down_w, down_b, ln_w, ln_b):
        import jax, jax.numpy as jnp
        import numpy as np
        D_MODEL, STATE, N_EXP, VOCAB = (128, 16, 4, 4000)
        B, L = (4, 256)
        EPS = 1e-05
        Bb, Ll, d = x.shape
        delta = jax.nn.softplus(jnp.einsum('bld,de->ble', x, Wd) + bd)
        Bm = jnp.einsum('bld,ds->bls', x, WB) + bB
        Cm = jnp.einsum('bld,ds->bls', x, WC) + bC
        A = -jnp.exp(A_log)

        def step(h, inps):
            x_t, d_t, B_t, C_t = inps
            bar_A = jnp.exp(jnp.minimum(d_t[:, :, None] * A, 2.0))
            bar_B = jnp.clip(d_t[:, :, None] * B_t[:, None, :], -2.0, 2.0)
            h = jnp.clip(bar_A * h + bar_B * x_t[:, :, None], -100.0, 100.0)
            y = jnp.sum(h * C_t[:, None, :], axis=-1) + x_t * D_param
            return (h, y)
        h0 = jnp.zeros((Bb, d, STATE), x.dtype)
        xs = (jnp.swapaxes(x, 0, 1), jnp.swapaxes(delta, 0, 1), jnp.swapaxes(Bm, 0, 1), jnp.swapaxes(Cm, 0, 1))
        _, ys = jax.lax.scan(step, h0, xs)
        ssm_out = jnp.swapaxes(ys, 0, 1)
        flat = ssm_out.reshape(-1, d)
        routing = jax.nn.softmax(flat @ Wr + br, axis=1)
        top1_w = jnp.max(routing, axis=1)
        top1_i = jnp.argmax(routing, axis=1)
        hid = jax.nn.silu(jnp.einsum('nd,edf->enf', flat, up_w) + up_b[:, None, :])
        all_out = jnp.einsum('enf,efd->end', hid, down_w) + down_b[:, None, :]
        sel = jnp.take_along_axis(jnp.swapaxes(all_out, 0, 1), top1_i[:, None, None], axis=1)[:, 0, :]
        moe_out = (sel * top1_w[:, None]).reshape(Bb, Ll, d)
        out = ssm_out + moe_out
        mu = jnp.mean(out, axis=-1, keepdims=True)
        var = jnp.mean((out - mu) ** 2, axis=-1, keepdims=True)
        return (out - mu) * jax.lax.rsqrt(var + EPS) * ln_w + ln_b

    def _L0_ffn_ref(x, w_gate, w_up, w_down):
        import jax, jax.numpy as jnp
        import numpy as np
        DIM = 128
        HIDDEN = 384
        SCALE = 1.0 / 127.0

        def _dequant(w_int, dtype):
            return w_int.astype(dtype) * jnp.asarray(SCALE, dtype)
        wg = _dequant(w_gate, x.dtype)
        wu = _dequant(w_up, x.dtype)
        wd = _dequant(w_down, x.dtype)
        gate = jnp.einsum('bsd,hd->bsh', x, wg)
        up = jnp.einsum('bsd,hd->bsh', x, wu)
        h = jax.nn.silu(gate) * up
        return jnp.einsum('bsh,dh->bsd', h, wd)
    x = L0_attn_x
    x = _layernorm(x + _L0_attn_ref(x, L0_attn_A_log, L0_attn_D_param, L0_attn_Wd, L0_attn_bd, L0_attn_WB, L0_attn_bB, L0_attn_WC, L0_attn_bC, L0_attn_Wr, L0_attn_br, L0_attn_up_w, L0_attn_up_b, L0_attn_down_w, L0_attn_down_b, L0_attn_ln_w, L0_attn_ln_b), axis=-1)
    x = _layernorm(x + _L0_ffn_ref(x, L0_ffn_w_gate, L0_ffn_w_up, L0_ffn_w_down), axis=-1)
    return x

_drawn_inputs = setup_inputs


def setup_inputs(seed=0):
    import zlib

    import numpy as np

    out = dict(_drawn_inputs(seed))
    spreads = {'L0_attn_D_param': (1.0, 0.2),
     'L0_attn_bd': (0.0, 0.686),
     'L0_attn_bB': (0.0, 0.1),
     'L0_attn_bC': (0.0, 0.1),
     'L0_attn_br': (0.0, 0.394),
     'L0_attn_up_b': (0.0, 0.8),
     'L0_attn_down_b': (0.0, 0.33),
     'L0_attn_ln_w': (1.0, 0.2),
     'L0_attn_ln_b': (0.0, 0.1)}
    factors = {'L0_attn_Wr': 2.718, 'L0_attn_up_w': 4.338, 'L0_attn_down_w': 3.994}
    for name, (base, spread) in spreads.items():
        noise = np.random.default_rng([zlib.crc32(name.encode()), seed]).standard_normal(out[name].shape)
        drawn = base * np.exp(spread * noise) if base else spread * noise
        out[name] = jnp.asarray(drawn.astype(out[name].dtype))
    for name, factor in factors.items():
        out[name] = (out[name] * factor).astype(out[name].dtype)
    return out
```

```python
from contextlib import ExitStack

import numpy as np

import concourse.bass as bass
from concourse import mybir

F32 = mybir.dt.float32
F32R = mybir.dt.float32r
BF16 = mybir.dt.bfloat16
I32 = mybir.dt.int32
ALU = mybir.AluOpType
ACT = mybir.ActivationFunctionType
X = mybir.AxisListType.X

NB, L, D = 8, 1024, 128
S = 16
E, F = 4, 512
NF = F // 128
H = 384
NH = H // 128
HALF = 512
NJ = HALF // 128
EPS = 1e-5
INV127 = 1.0 / 127.0
CLIP_B, CLIP_H = 2.0, 100.0
SAFE_B, SAFE_H = 1.98, 90.0
NDECAY = 8
NPROD = 2
FIRST_FULL, LAST_FULL = 2, 6

PE_STEPS = [
    (0, "B", "y_turn"), (1, "B", "router"), (2, "C", "x_turn", 1), (3, "B", "up", 0), (4, "C", "ff_up", 1),
    (5, "B", "up", 1), (6, "B", "down", 0), (7, "B", "up", 2), (8, "C", "ff_down", 1), (9, "B", "down", 1),
    (10, "B", "up", 3), (11, "B", "down", 2), (12, "B", "up", 4), (13, "B", "down", 3), (14, "B", "up", 5),
    (15, "B", "down", 4), (16, "P", "z"), (17, "B", "up", 6), (18, "B", "down", 5), (19, "P", "bc"),
    (20, "B", "up", 7), (20, "P", "b_turn"), (21, "B", "down", 6), (22, "B", "x_turn", 0), (23, "B", "down", 7),
    (24, "B", "ff_up", 0), (25, "P", "b_spread", 0), (26, "P", "b_spread", 1), (27, "B", "ff_down", 0),
    (31, "P", "flag"),
]
ACT_STEPS = [
    (0, "B", "y_copy"), (0, "A", "decay", 0), (2, "B", "router_exp"), (3, "C", "x_high", 1), (3, "B", "silu", 0),
    (4, "C", "gate", 1), (5, "B", "silu", 1), (6, "A", "decay", 1), (7, "B", "silu", 2), (10, "B", "silu", 3),
    (12, "B", "silu", 4), (13, "A", "decay", 2), (14, "B", "silu", 5), (16, "P", "z_copy"), (17, "B", "silu", 6),
    (19, "P", "bc_copy"), (20, "B", "silu", 7), (21, "A", "decay", 3), (21, "P", "softplus"), (22, "P", "bc_mid"),
    (22, "B", "x_high", 0), (24, "B", "gate", 0), (25, "P", "x_scaled"), (27, "P", "decay_bound"),
]
DVE_STEPS = [
    (2, "B", "router_shift"), (3, "C", "x_low", 1), (4, "B", "router_pick"), (5, "C", "ff_mul", 1),
    (7, "B", "weigh", 0), (9, "C", "ff_sum", 1), (10, "B", "weigh", 1), (10, "C", "norm", 1, 2),
    (12, "B", "weigh", 2), (14, "B", "weigh", 3), (15, "B", "stats", 0, 0), (16, "B", "norm", 0, 0),
    (16, "B", "weigh", 4), (19, "B", "weigh", 5), (19, "B", "stats", 0, 1), (20, "B", "norm", 0, 1),
    (22, "P", "b_max"), (22, "B", "weigh", 6), (23, "B", "x_low", 0), (23, "P", "delta"), (24, "B", "weigh", 7), (24, "P", "bc_low"),
    (25, "B", "stats", 1, 0), (25, "B", "ff_mul", 0), (26, "B", "norm", 1, 0), (26, "P", "bound", 0),
    (27, "P", "bound", 1), (28, "B", "ff_sum", 0), (29, "B", "stats", 1, 1), (30, "B", "norm", 1, 1),
    (30, "P", "majorant"), (31, "B", "norm", 0, 2), (31, "P", "flag"),
]
POOL_STEPS = [
    (8, "B", "mix", 0), (9, "C", "rstd", 1, 2), (11, "B", "mix", 1), (13, "B", "mix", 2), (14, "B", "mix", 3),
    (15, "B", "rstd", 0, 0), (16, "B", "affine", 0), (17, "B", "mix", 4), (19, "B", "rstd", 0, 1), (20, "B", "mix", 5),
    (20, "P", "bc_rest"), (23, "B", "mix", 6), (24, "B", "mix", 7), (25, "B", "rstd", 1, 0),
    (26, "B", "affine", 1), (28, "P", "bound_input"), (28, "B", "rstd", 0, 2), (29, "B", "rstd", 1, 1),
]
FILLS = {
    "z": ["U0", "U1"], "bc": ["U0", "U1"], "up": ["U0", "U1", "U0", "U1"], "ff_up": ["U0", "U1"] * NH,
    "down": ["D"], "ff_down": ["D"], "y_turn": ["T", "T"], "router": ["T"], "x_turn": ["T"],
    "b_turn": ["T"], "b_spread": ["T"], "flag": ["T"],
}


class Iteration:

    def __init__(self, i):
        full = not isinstance(i, int)
        offset = {"P": 1, "A": 0, "B": -1, "C": -2}
        self.b, self.runs, self.ran = {}, {}, {}
        for stage, d in offset.items():
            self.b[stage] = i + d
            self.runs[stage] = full or 0 <= i + d < NB
            self.ran[stage] = i + d if full else min(max(i + d, 0), NB)

    def tasks(self, steps, step):
        return [t[1:] for t in steps if t[0] == step and self.runs[t[1]]]

    def fills(self, bank, stage, task, k=0):
        before, count = 0, None
        per = {"P": 0, "B": 0, "C": 0}
        for t in PE_STEPS:
            n = sum(x == bank for x in FILLS[t[2]])
            per[t[1]] += n
            if t[1:] == (stage, *task):
                count = before + k + 1
            if self.runs[t[1]]:
                before += n
        assert count is not None
        return sum(per[s] * self.ran[s] for s in per) + count


def ssm_moe_ffn_kernel(nc, xT, x, a_log, d_param, wd, bd, wbc, bbc, wr, br, up_w, up_b, down_w, down_b,
                       ln_w, ln_b, wg, wu, wdn, ident_c, sel_c, rev_c, out):
    ctx = ExitStack()
    with ctx:
        def sb(name, shape, dt=F32):
            return ctx.enter_context(nc.sbuf_tensor(name, shape, dt))

        def pb(name, shape, dt=F32):
            return ctx.enter_context(nc.psum_tensor(name, shape, dt))

        def sem(name):
            return ctx.enter_context(nc.semaphore(name))

        wd_sb = sb("wd_sb", [D, D])
        wbc_sb = sb("wbc_sb", [D, 128])
        wr_sb = sb("wr_sb", [D, E])
        up_sb = sb("up_sb", [D, E, F])
        down_sb = sb("down_sb", [128, E * NF, D])
        wg_sb = sb("wg_sb", [D, H], F32R)
        wu_sb = sb("wu_sb", [D, H], F32R)
        wdn_sb = sb("wdn_sb", [128, NH, D])
        a_sb = sb("a_sb", [D, S])
        a_max = sb("a_max", [D, 1])
        dpar = sb("dpar", [D, 1])
        bd_sb = sb("bd_sb", [D, 1])
        bbc_sb = sb("bbc_sb", [128, 1])
        upb_sb = sb("upb_sb", [128, E * NF])
        br_sb = sb("br_sb", [128, E])
        rev_sb = sb("rev_sb", [128, E])
        lnw_sb = sb("lnw_sb", [128, D])
        lnb_sb = sb("lnb_sb", [128, D])
        ident = sb("ident", [128, 128])
        identb = sb("identb", [128, 128], BF16)
        selcol = sb("selcol", [128, 2 * S])
        sel = sb("sel", [128, 2 * S, 128], BF16)
        bias_down = sb("bias_down", [128, E, NJ, D], BF16)
        ones_col = sb("ones_col", [128, 1])
        minus_half = sb("minus_half", [128, NJ])
        limits = sb("limits", [128, 3])
        xT_sb = sb("xT_sb", [D, L])
        zb = sb("zb", [D, L])
        sp = sb("sp", [D, L])
        bcf = sb("bcf", [128, L])
        rest = sb("rest", [128, L])
        parts = sb("parts", [128, L], BF16)
        bmax = sb("bmax", [128, 2 * NJ], BF16)
        next_delta = sb("next_delta", [D, L])
        amx = sb("amx", [D, L])
        x_abs = sb("x_abs", [D, L])
        bnd = sb("bnd", [D, L])
        xD = sb("xD", [D, L])
        peak = sb("peak", [D, 3])
        over = sb("over", [D, 3])
        holder = sb("holder", [128, 1])
        clip_flag = sb("clip_flag", [1, 1], I32)
        bc_parts = sb("bc_parts", [128, L], BF16)
        delta = sb("delta", [D, L])
        dx = sb("dx", [D, L])
        x_again = sb("x_again", [D, L])
        decay = sb("decay", [D, NDECAY, L])
        inp = sb("inp", [D, L])
        state = sb("state", [D, L])
        prod = sb("prod", [D, NPROD, L])
        yacc = sb("yacc", [D, L])
        y = sb("y", [D, L])
        xt = sb("xt", [128, 2, NJ, D])
        ytok = sb("ytok", [128, 2, HALF])
        rs = sb("rs", [128, 2 * NJ, E])
        ex = sb("ex", [128, 2 * NJ, E])
        rsmall = sb("rsmall", [128, 4, 2 * NJ])
        rcode = sb("rcode", [128, 2 * NJ, E])
        top_w = sb("top_w", [128, 2 * NJ, E])
        hid = sb("hid", [128, 2, NF, HALF])
        weighed = sb("weighed", [128, 2, NJ, D])
        moe = sb("moe", [128, 2, NJ, D])
        attn = sb("attn", [128, 2, NJ, D])
        x1 = sb("x1", [128, 2, NJ, D])
        x1h = sb("x1h", [D, HALF], F32R)
        x1l = sb("x1l", [D, HALF], F32R)
        hh = sb("hh", [128, NH, HALF])
        x2 = sb("x2", [128, 2, NJ, D])
        bst = sb("bst", [128, 2, NJ, 6])
        mv = sb("mv", [128, 2, NJ, 2])
        ve = sb("ve", [128, 2, NJ])
        rstd = sb("rstd", [128, 2, NJ])

        psB = pb("psB", [D, L])
        psC = pb("psC", [D, L])
        bank = {n: pb("ps" + n, [128, HALF]) for n in ("U0", "U1", "D", "T")}
        filled = {n: sem(f"filled_{n}") for n in bank}
        drained = {n: sem(f"drained_{n}") for n in bank}

        consts_in = sem("consts_in")
        bias_rows_in = sem("bias_rows_in")
        ff_in = sem("ff_in")
        setup_dve = sem("setup_dve")
        setup_act = sem("setup_act")
        consts_ready = sem("consts_ready")
        xT_in = sem("xT_in")
        x_again_in = sem("x_again_in")
        xt_in = [sem(f"xt_in{c}") for c in range(2)]
        out_done = [sem(f"out_done{c}") for c in range(2)]
        parts_high = sem("parts_high")
        rest_ready = sem("rest_ready")
        parts_mid = sem("parts_mid")
        parts_ready = sem("parts_ready")
        softplus_steps = sem("softplus_steps")
        delta_next = sem("delta_next")
        x_scaled = sem("x_scaled")
        amx_ready = sem("amx_ready")
        bnd_ready = sem("bnd_ready")
        flag_steps = sem("flag_steps")
        bc_parts_ready = sem("bc_parts_ready")
        delta_ready = sem("delta_ready")
        dx_ready = sem("dx_ready")
        b_ready = sem("b_ready")
        c_ready = sem("c_ready")
        decay_ready = sem("decay_ready")
        inp_ready = sem("inp_ready")
        state_ready = sem("state_ready")
        prod_ready = sem("prod_ready")
        added = sem("added")
        slow_steps = sem("slow_steps")
        stats_local = sem("stats_local")
        router_steps = sem("router_steps")
        router_exp = sem("router_exp")
        mixed = sem("mixed")
        stats_steps = [sem(f"stats_steps{c}") for c in range(2)]
        rstd_ready = [sem(f"rstd_ready{c}") for c in range(2)]
        normed = [sem(f"normed{c}") for c in range(2)]
        affine_steps = [sem(f"affine_steps{c}") for c in range(2)]
        x_high = [sem(f"x_high{c}") for c in range(2)]

        def wait(eng, s, value):
            if not isinstance(value, int) or value > 0:
                eng.wait_ge(s, value)

        def wait_apart(eng, s, value):
            eng.wait_ge(consts_in, 16)
            wait(eng, s, value)

        def iterate(eng, body):
            for i in range(-1, FIRST_FULL):
                body(Iteration(i))
            with eng.Fori(FIRST_FULL, LAST_FULL + 1) as i:
                body(Iteration(i))
            for i in range(LAST_FULL + 1, NB + 2):
                body(Iteration(i))

        def half(t, c):
            return t[:, c * HALF:(c + 1) * HALF]

        def by_token(n):
            return bank[n][:, :].rearrange("p (j d) -> p j d", j=NJ)

        block = ctx.enter_context(nc.Block())

        @block.sync
        def _(sp_):
            for dst, src in (
                (wd_sb[:, :], wd), (wbc_sb[:, :], wbc), (bd_sb[:, :], bd), (bbc_sb[:, :], bbc),
                (a_sb[:, :], a_log), (dpar[:, :], d_param), (wr_sb[:, :], wr), (ident[:, :], ident_c),
                (selcol[:, :], sel_c), (rev_sb[:, :], rev_c.to_broadcast([128, E])),
                (br_sb[:, :], br.to_broadcast([128, E])),
                (lnw_sb[:, :], ln_w.to_broadcast([128, D])), (lnb_sb[:, :], ln_b.to_broadcast([128, D])),
                (upb_sb[:, :], up_b), (up_sb[:, :, :], up_w.rearrange("e d f -> d e f")),
                (down_sb[:, :, :], down_w.rearrange("e (n p) d -> p (e n) d", p=128)),
            ):
                sp_.dma_start(dst, src).then_inc(consts_in, 16)
            stage = hid[:, 0, :, :].rearrange("p n t -> p (n t)").bitcast(I32)
            for k, w in enumerate((wg, wu, wdn)):
                dst = stage[:, k * H:(k + 1) * H]
                if k == 2:
                    dst = dst.rearrange("p (m d) -> p m d", m=NH)
                    w = w.rearrange("(m p) d -> p m d", p=128)
                sp_.dma_start(dst, w).then_inc(ff_in, 16)
            sp_.wait_ge(setup_dve, 1)
            for row in (0, 64, 96):
                sp_.dma_start(rest[row:row + 1, 0:E * D], down_b).then_inc(bias_rows_in, 16)

            def body(it):
                if it.runs["P"]:
                    b = it.b["P"]
                    wait(sp_, x_scaled, 2 * b)
                    wait(sp_, dx_ready, b)
                    sp_.dma_start(xT_sb[:, :], xT[b]).then_inc(xT_in, 16)
                if it.runs["A"]:
                    b = it.b["A"]
                    wait(sp_, prod_ready, S * b)
                    wait(sp_, x_again_in, 16 * b)
                    sp_.dma_start(x_again[:, :], xT[b]).then_inc(x_again_in, 16)
                if it.runs["B"]:
                    b = it.b["B"]
                    for c in range(2):
                        wait(sp_, affine_steps[c], 3 * b)
                        sp_.dma_start(xt[:, c, :, :], x[b].rearrange("(c j p) d -> c p j d", p=128, c=2)[c]
                                      ).then_inc(xt_in[c], 16)
                if it.runs["C"]:
                    b = it.b["C"]
                    wait(sp_, normed[1], 3 * b + 3)
                    sp_.dma_start(out[b].rearrange("(c j p) d -> c p j d", p=128, c=2)[1], x2[:, 1, :, :]
                                  ).then_inc(out_done[1], 16)
                if it.runs["B"]:
                    b = it.b["B"]
                    wait(sp_, normed[0], 3 * b + 3)
                    sp_.dma_start(out[b].rearrange("(c j p) d -> c p j d", p=128, c=2)[0], x2[:, 0, :, :]
                                  ).then_inc(out_done[0], 16)

            iterate(sp_, body)
            for c in range(2):
                sp_.wait_ge(out_done[c], 16 * NB)
            sp_.wait_ge(x_again_in, 16 * NB)

        @block.tensor
        def _(pe):
            def scan_operand(it, s, which):
                b = it.b["A"]
                ps, ready, used = (psB, b_ready, inp_ready) if which == 0 else (psC, c_ready, prod_ready)
                wait(pe, used, S * b + s)
                if which == 0 and s == 0:
                    wait(pe, bc_parts_ready, b + 1)
                for c in range(2):
                    mm = pe.matmul(half(ps, c), sel[:, which * S + s, :], half(bc_parts, c), start=True, stop=True)
                mm.then_inc(ready, 1)

            def fill(it, name, stage, task, k=0):
                wait(pe, drained[name], it.fills(name, stage, task, k) - 1)

            def run(it, stage, name, *args):
                b = it.b[stage]
                task = (name, *args)
                banks = FILLS[name]
                if name in ("z", "bc"):
                    wait(pe, xT_in, 16 * (b + 1))
                    for c in range(2):
                        fill(it, banks[c], stage, task)
                        pe.matmul(bank[banks[c]][:, :], (wd_sb if name == "z" else wbc_sb)[:, :], half(xT_sb, c),
                                  start=True, stop=True).then_inc(filled[banks[c]], 1)
                if name == "b_turn":
                    wait_apart(pe, drained["U1"], it.fills("U1", "P", ("bc",)))
                    fill(it, "T", stage, task)
                    for j in range(2 * NJ):
                        mm = pe.transpose(bank["T"][:, j * 32:j * 32 + 32], bcf[0:32, j * 128:(j + 1) * 128],
                                          ident[0:32, 0:32])
                    mm.then_inc(filled["T"], 1)
                if name == "b_spread":
                    (c,) = args
                    wait(pe, drained["T"], it.fills("T", "P", ("b_turn",)))
                    fill(it, "T", stage, task)
                    for j in range(NJ):
                        mm = pe.matmul(bank["T"][:, j * 128:(j + 1) * 128],
                                       bmax[:, c * NJ + j:c * NJ + j + 1].to_broadcast([128, 128]), identb[:, :],
                                       start=True, stop=True)
                    mm.then_inc(filled["T"], 1)
                if name == "flag":
                    wait(pe, flag_steps, 3 * b + 3)
                    fill(it, "T", stage, task)
                    pe.matmul(bank["T"][0:1, 0:3], ones_col[:, :], over[:, :], start=True, stop=True
                              ).then_inc(filled["T"], 1)
                if name == "y_turn":
                    wait(pe, added, S * (b + 1))
                    for c in range(2):
                        fill(it, "T", stage, task, c)
                        for j in range(NJ):
                            t = (c * NJ + j) * 128
                            mm = pe.transpose(bank["T"][:, j * 128:(j + 1) * 128], y[:, t:t + 128], ident[:, :])
                        mm.then_inc(filled["T"], 1)
                if name == "router":
                    fill(it, "T", stage, task)
                    for j in range(2 * NJ):
                        mm = pe.matmul(bank["T"][:, j * E:(j + 1) * E], y[:, j * 128:(j + 1) * 128], wr_sb[:, :],
                                       start=True, stop=True)
                    mm.then_inc(filled["T"], 1)
                if name == "up":
                    c, e = divmod(args[0], E)
                    for f in range(NF):
                        fill(it, banks[f], stage, task, f // 2)
                        pe.matmul(bank[banks[f]][:, :], up_sb[:, e, f * 128:(f + 1) * 128], half(y, c),
                                  start=True, stop=True).then_inc(filled[banks[f]], 1)
                if name == "down":
                    k = args[0]
                    e = k % E
                    fill(it, "D", stage, task)
                    pe.matmul(bank["D"][:, :], sel[:, 0, :],
                              bias_down[:, e, :, :].rearrange("p j d -> p (j d)"), start=True, stop=False,
                              skip_group_check=True)
                    for u in ("U0", "U1"):
                        wait(pe, drained[u], it.fills(u, "B", ("up", k), 1))
                    for j in range(NJ):
                        for f in range(NF):
                            mm = pe.matmul(bank["D"][:, j * 128:(j + 1) * 128],
                                           hid[:, k % 2, f, j * 128:(j + 1) * 128], down_sb[:, e * NF + f, :],
                                           start=False, stop=(f == NF - 1), skip_group_check=True)
                    mm.then_inc(filled["D"], 1)
                if name == "x_turn":
                    (c,) = args
                    wait(pe, normed[c], 3 * b + 2)
                    fill(it, "T", stage, task)
                    for j in range(NJ):
                        mm = pe.transpose(bank["T"][:, j * 128:(j + 1) * 128], x1[:, c, j, :], ident[:, :])
                    mm.then_inc(filled["T"], 1)
                if name == "ff_up":
                    (c,) = args
                    wait(pe, drained["T"], it.fills("T", stage, ("x_turn", c)))
                    for m in range(NH):
                        for u, w in (("U0", wg_sb), ("U1", wu_sb)):
                            fill(it, u, stage, task, m)
                            pe.matmul(bank[u][:, :], w[:, m * 128:(m + 1) * 128], x1h[:, :], start=True, stop=False)
                            pe.matmul(bank[u][:, :], w[:, m * 128:(m + 1) * 128], x1l[:, :], start=False, stop=True
                                      ).then_inc(filled[u], 1)
                if name == "ff_down":
                    (c,) = args
                    wait(pe, drained["U1"], it.fills("U1", stage, ("ff_up", c), NH - 1))
                    fill(it, "D", stage, task)
                    for j in range(NJ):
                        for m in range(NH):
                            mm = pe.matmul(bank["D"][:, j * 128:(j + 1) * 128], hh[:, m, j * 128:(j + 1) * 128],
                                           wdn_sb[:, m, :], start=(m == 0), stop=(m == NH - 1),
                                           skip_group_check=True)
                    mm.then_inc(filled["D"], 1)

            def body(it):
                for s in range(S):
                    if it.runs["A"]:
                        if s == 0:
                            scan_operand(it, 0, 0)
                        scan_operand(it, s, 1)
                    for t in it.tasks(PE_STEPS, 2 * s):
                        run(it, *t)
                    if it.runs["A"] and s + 1 < S:
                        scan_operand(it, s + 1, 0)
                    for t in it.tasks(PE_STEPS, 2 * s + 1):
                        run(it, *t)

            pe.wait_ge(consts_in, 16 * 16)
            pe.wait_ge(consts_ready, 2)
            iterate(pe, body)

        @block.scalar
        def _(act):
            act.wait_ge(consts_in, 16 * 16)
            nc.scalar.activation(a_sb[:, :], a_sb[:, :], ACT.Exp).then_inc(setup_act, 1)
            act.wait_ge(setup_act, 1)
            nc.scalar.activation(a_sb[:, :], a_sb[:, :], ACT.Copy, scale=-1.0).then_inc(consts_ready, 1)
            act.wait_ge(consts_ready, 2)

            def run(it, stage, name, *args):
                b = it.b[stage]
                if name == "z_copy":
                    wait(act, delta_next, b)
                    for c, u in enumerate(("U0", "U1")):
                        act.wait_ge(filled[u], it.fills(u, "P", ("z",)))
                        nc.scalar.activation(half(zb, c), bank[u][:, :], ACT.Identity, bias=bd_sb[:, 0:1]
                                             ).then_inc(drained[u], 1)
                if name == "bc_copy":
                    wait(act, parts_ready, b)
                    wait(act, delta_next, b)
                    for c, u in enumerate(("U0", "U1")):
                        act.wait_ge(filled[u], it.fills(u, "P", ("bc",)))
                        nc.scalar.activation(half(bcf, c), bank[u][:, :], ACT.Identity, bias=bbc_sb[:, 0:1]
                                             ).then_inc(drained[u], 1)
                    wait(act, bc_parts_ready, b)
                    for u in ("U0", "U1"):
                        act.wait_ge(drained[u], it.fills(u, "P", ("bc",)))
                    nc.scalar.activation(parts[:, :], bcf[:, :], ACT.Copy).then_inc(parts_high, 1)
                if name == "bc_mid":
                    act.wait_ge(rest_ready, b + 1)
                    nc.scalar.activation(parts[64:128, :], rest[64:128, :], ACT.Copy).then_inc(parts_mid, 1)
                if name == "softplus":
                    wait(act, delta_next, b)
                    for u in ("U0", "U1"):
                        act.wait_ge(drained[u], it.fills(u, "P", ("z",)))
                    nc.scalar.activation(sp[:, :], zb[:, :], ACT.Abs).then_inc(softplus_steps, 1)
                    act.wait_ge(softplus_steps, 3 * b + 1)
                    nc.scalar.activation(sp[:, :], sp[:, :], ACT.Exp, scale=-1.0).then_inc(softplus_steps, 1)
                    act.wait_ge(softplus_steps, 3 * b + 2)
                    nc.scalar.activation(sp[:, :], sp[:, :], ACT.Ln, bias=1.0).then_inc(softplus_steps, 1)
                if name == "x_scaled":
                    act.wait_ge(xT_in, 16 * (b + 1))
                    wait(act, bnd_ready, 2 * b)
                    nc.scalar.activation(x_abs[:, :], xT_sb[:, :], ACT.Abs).then_inc(x_scaled, 1)
                    wait(act, added, S * (b - 1) + 1)
                    nc.scalar.activation(xD[:, :], xT_sb[:, :], ACT.Copy, scale=dpar[:, 0:1]).then_inc(x_scaled, 1)
                if name == "decay_bound":
                    act.wait_ge(delta_next, b + 1)
                    wait(act, flag_steps, 3 * b)
                    nc.scalar.activation(amx[:, :], next_delta[:, :], ACT.Exp, scale=a_max[:, 0:1]
                                         ).then_inc(amx_ready, 1)
                if name == "decay":
                    for s in range(4 * args[0], 4 * args[0] + 4):
                        if s == 0:
                            act.wait_ge(delta_ready, b + 1)
                        wait(act, state_ready, S * b + s - NDECAY + 1)
                        nc.scalar.activation(decay[:, s % NDECAY, :], delta[:, :], ACT.Exp, scale=a_sb[:, s:s + 1]
                                             ).then_inc(decay_ready, 1)
                if name == "y_copy":
                    wait(act, mixed, 8 * b)
                    for c in range(2):
                        act.wait_ge(filled["T"], it.fills("T", "B", ("y_turn",), c))
                        nc.scalar.activation(ytok[:, c, :], bank["T"][:, :], ACT.Copy).then_inc(drained["T"], 1)
                if name == "router_exp":
                    act.wait_ge(router_steps, 8 * b + 3)
                    nc.scalar.activation(ex[:, :, :], rs[:, :, :], ACT.Exp).then_inc(router_exp, 1)
                if name == "silu":
                    k = args[0]
                    for f in range(NF):
                        u = FILLS["up"][f]
                        act.wait_ge(filled[u], it.fills(u, "B", ("up", k), f // 2))
                        nc.scalar.activation(hid[:, k % 2, f, :], bank[u][:, :], ACT.Silu,
                                             bias=upb_sb[:, (k % E) * NF + f:(k % E) * NF + f + 1]
                                             ).then_inc(drained[u], 1)
                if name == "x_high":
                    (c,) = args
                    act.wait_ge(filled["T"], it.fills("T", stage, ("x_turn", c)))
                    nc.scalar.activation(x1h[:, :], bank["T"][:, :], ACT.Copy).then_inc(x_high[c], 1)
                if name == "gate":
                    (c,) = args
                    for m in range(NH):
                        act.wait_ge(filled["U0"], it.fills("U0", stage, ("ff_up", c), m))
                        nc.scalar.activation(hh[:, m, :], bank["U0"][:, :], ACT.Silu, scale=INV127
                                             ).then_inc(drained["U0"], 1)

            def body(it):
                for step in range(2 * S):
                    for t in it.tasks(ACT_STEPS, step):
                        run(it, *t)

            iterate(act, body)

        @block.vector
        def _(dve):
            v = nc.vector
            steps = [0]

            def setup(ins):
                steps[0] += 1
                ins.then_inc(setup_dve, 1)
                dve.wait_ge(setup_dve, steps[0])

            setup(v.memset(rest[:, 0:E * D], 0.0))
            setup(v.memset(ones_col[:, :], 1.0))
            setup(v.memset(minus_half[:, :], -0.5))
            setup(v.memset(limits[:, 0:2], SAFE_B))
            setup(v.memset(limits[:, 2:3], SAFE_H))
            dve.wait_ge(consts_in, 16 * 16)
            setup(v.tensor_copy(identb[:, :], ident[:, :]))
            setup(v.tensor_copy(sel[:, :, :], selcol[:, :].rearrange("p (s o) -> p s o", o=1).to_broadcast([128, 2 * S, 128])))
            dve.wait_ge(ff_in, 48)
            stage = hid[:, 0, :, :].rearrange("p n t -> p (n t)").bitcast(I32)
            setup(v.tensor_copy(wg_sb[:, :], stage[:, 0:H]))
            setup(v.tensor_copy(wu_sb[:, :], stage[:, H:2 * H]))
            setup(v.tensor_copy(wdn_sb[:, :, :].rearrange("p m d -> p (m d)"), stage[:, 2 * H:3 * H]))
            dve.wait_ge(bias_rows_in, 48)
            row = rest[:, 0:E * D]
            part = inp[:, 0:E * D // 2].bitcast(BF16)
            setup(v.tensor_copy(part, row))
            setup(v.tensor_tensor(row[64:128, :], row[64:128, :], part[64:128, :], ALU.subtract))
            setup(v.tensor_copy(part[64:128, :], row[64:128, :]))
            setup(v.tensor_tensor(part[96:128, :], row[96:128, :], part[96:128, :], ALU.subtract))
            for j in range(NJ):
                setup(v.tensor_copy(bias_down[:, :, j, :], part.rearrange("p (e d) -> p e d", e=E)))
            dve.wait_ge(consts_ready, 1)
            setup(v.tensor_reduce(a_max[:, :], a_sb[:, :], X, ALU.max))
            v.memset(peak[:, :], 0.0).then_inc(consts_ready, 1)
            dve.wait_ge(consts_ready, 2)

            def wide(t, n, d):
                return t.rearrange("p (n o) -> p n o", o=1).to_broadcast([128, n, d])

            def fast_input(s):
                v.tensor_tensor(inp[:, :], dx[:, :], psB[:, :], ALU.mult).then_inc(inp_ready, 1)

            def slow_input(b, s):
                dve.wait_ge(x_again_in, 16 * (b + 1))
                v.tensor_tensor(inp[:, :], delta[:, :], psB[:, :], ALU.mult).then_inc(slow_steps, 1)
                dve.wait_ge(slow_steps, 1)
                v.tensor_scalar(inp[:, :], inp[:, :], CLIP_B, -CLIP_B, ALU.min, ALU.max).then_inc(slow_steps, 1)
                dve.wait_ge(slow_steps, 2)
                dve.sem_clear(slow_steps)
                v.tensor_tensor(inp[:, :], inp[:, :], x_again[:, :], ALU.mult).then_inc(inp_ready, 1)

            def slow_scan(s):
                a = decay[:, s % NDECAY, :]

                def step(now, before):
                    if before is None:
                        v.tensor_copy(state[:, now], inp[:, now]).then_inc(slow_steps, 1)
                    else:
                        v.scalar_tensor_tensor(out=state[:, now], in0=a[:, now], scalar=state[:, before],
                                               in1=inp[:, now], op0=ALU.mult, op1=ALU.add).then_inc(slow_steps, 1)
                    dve.wait_ge(slow_steps, 1)
                    v.tensor_scalar(state[:, now], state[:, now], CLIP_H, -CLIP_H, ALU.min, ALU.max
                                    ).then_inc(slow_steps, 1)
                    dve.wait_ge(slow_steps, 2)
                    dve.sem_clear(slow_steps)

                step(slice(0, 1), None)
                with dve.Fori(1, L) as t:
                    step(bass.ds(t, 1), bass.ds(t - 1, 1))
                v.tensor_copy(state[:, L - 1:L], state[:, L - 1:L]).then_inc(state_ready, 1)

            def run(it, stage, name, *args):
                b = it.b[stage]
                if name == "b_max":
                    dve.wait_ge(filled["T"], it.fills("T", "P", ("b_turn",)))
                    v.tensor_reduce(bmax[:, :], bank["T"][:, 0:64 * NJ].rearrange("p (j s) -> p j s", s=32)[:, :, 0:S],
                                    X, ALU.max, apply_absolute_value=True).then_inc(drained["T"], 1)
                if name == "delta":
                    dve.wait_ge(softplus_steps, 3 * (b + 1))
                    wait(dve, amx_ready, b)
                    v.scalar_tensor_tensor(out=next_delta[:, :], in0=zb[:, :], scalar=0.0, in1=sp[:, :],
                                           op0=ALU.max, op1=ALU.add).then_inc(delta_next, 1)
                if name == "bc_low":
                    dve.wait_ge(parts_mid, b + 1)
                    v.tensor_tensor(parts[96:128, :], rest[96:128, :], parts[96:128, :], ALU.subtract
                                    ).then_inc(parts_ready, 1)
                if name == "bound":
                    (c,) = args
                    dve.wait_ge(delta_next, b + 1)
                    dve.wait_ge(filled["T"], it.fills("T", "P", ("b_spread", c)))
                    v.memset(holder[:, :], 0.0)
                    v.tensor_tensor_reduce(half(bnd, c), half(next_delta, c), bank["T"][:, :], 1.0, 0.0,
                                           ALU.mult, ALU.max, peak[:, c:c + 1]).then_inc(drained["T"], 1)
                if name == "majorant":
                    dve.wait_ge(amx_ready, b + 1)
                    dve.wait_ge(bnd_ready, 2 * (b + 1))
                    wait(dve, state_ready, S * b)
                    v.tensor_tensor_scan(inp[:, :], amx[:, :], bnd[:, :], 0.0, ALU.mult, ALU.add
                                         ).then_inc(flag_steps, 1)
                    dve.wait_ge(flag_steps, 3 * b + 1)
                    v.tensor_reduce(peak[:, 2:3], inp[:, :], X, ALU.max).then_inc(flag_steps, 1)
                    dve.wait_ge(flag_steps, 3 * b + 2)
                    dve.wait_ge(drained["T"], it.fills("T", "P", ("b_spread", 1)))
                    v.tensor_tensor(over[:, :], peak[:, :], limits[:, :], ALU.is_gt).then_inc(flag_steps, 1)
                if name == "flag":
                    dve.wait_ge(filled["T"], it.fills("T", "P", ("flag",)))
                    v.tensor_reduce(clip_flag[:, :], bank["T"][0:1, 0:3], X, ALU.max).then_inc(drained["T"], 1)
                    dve.wait_ge(drained["T"], it.fills("T", "P", ("flag",)))
                if name == "router_shift":
                    dve.wait_ge(filled["T"], it.fills("T", "B", ("router",)))
                    v.tensor_tensor(rs[:, :, :], bank["T"][:, 0:2 * NJ * E].rearrange("p (j e) -> p j e", e=E),
                                    br_sb[:, :].rearrange("p (o e) -> p o e", o=1).to_broadcast([128, 2 * NJ, E]),
                                    ALU.add).then_inc(drained["T"], 1)
                    dve.wait_ge(drained["T"], it.fills("T", "B", ("router",)))
                    v.tensor_reduce(rsmall[:, 0, :], rs[:, :, :], X, ALU.max).then_inc(router_steps, 1)
                    dve.wait_ge(router_steps, 8 * b + 1)
                    v.tensor_tensor(rs[:, :, :], rs[:, :, :], wide(rsmall[:, 0, :], 2 * NJ, E), ALU.subtract
                                    ).then_inc(router_steps, 1)
                    dve.wait_ge(router_steps, 8 * b + 2)
                    v.scalar_tensor_tensor(out=rcode[:, :, :], in0=rs[:, :, :], scalar=0.0,
                                           in1=rev_sb[:, :].rearrange("p (o e) -> p o e", o=1).to_broadcast([128, 2 * NJ, E]),
                                           op0=ALU.is_equal, op1=ALU.mult).then_inc(router_steps, 1)
                if name == "router_pick":
                    dve.wait_ge(router_steps, 8 * b + 3)
                    v.tensor_reduce(rsmall[:, 1, :], rcode[:, :, :], X, ALU.max).then_inc(router_steps, 1)
                    dve.wait_ge(router_exp, b + 1)
                    v.tensor_reduce(rsmall[:, 2, :], ex[:, :, :], X, ALU.add).then_inc(router_steps, 1)
                    dve.wait_ge(router_steps, 8 * b + 5)
                    v.reciprocal(rsmall[:, 3, :], rsmall[:, 2, :]).then_inc(router_steps, 1)
                    v.tensor_tensor(top_w[:, :, :], rcode[:, :, :], wide(rsmall[:, 1, :], 2 * NJ, E), ALU.is_equal
                                    ).then_inc(router_steps, 1)
                    dve.wait_ge(router_steps, 8 * b + 7)
                    v.tensor_tensor(top_w[:, :, :], top_w[:, :, :], wide(rsmall[:, 3, :], 2 * NJ, E), ALU.mult
                                    ).then_inc(router_steps, 1)
                if name == "weigh":
                    k = args[0]
                    c, e = divmod(k, E)
                    dve.wait_ge(filled["D"], it.fills("D", "B", ("down", k)))
                    dve.wait_ge(router_steps, 8 * (b + 1))
                    wait(dve, mixed, 8 * b + k - 1)
                    v.tensor_tensor(weighed[:, k % 2, :, :], by_token("D"),
                                    top_w[:, c * NJ:(c + 1) * NJ, e:e + 1].to_broadcast([128, NJ, D]), ALU.mult
                                    ).then_inc(drained["D"], 1)
                if name in ("stats", "ff_sum"):
                    c = args[0]
                    n = 2 if name == "ff_sum" else args[1]
                    if n == 0:
                        dve.wait_ge(mixed, 8 * b + 4 * (c + 1))
                        src = moe
                    elif n == 1:
                        dve.wait_ge(affine_steps[c], 3 * (b + 1))
                        src = attn
                    else:
                        dve.wait_ge(filled["D"], it.fills("D", stage, ("ff_down", c)))
                        wait(dve, out_done[c], 16 * b)
                        v.scalar_tensor_tensor(out=x2[:, c, :, :].rearrange("p j d -> p (j d)"), in0=bank["D"][:, :],
                                               scalar=INV127, in1=x1[:, c, :, :].rearrange("p j d -> p (j d)"),
                                               op0=ALU.mult, op1=ALU.add).then_inc(drained["D"], 1)
                        dve.wait_ge(drained["D"], it.fills("D", stage, ("ff_down", c)))
                        src = x2
                    for j in range(NJ):
                        ins = v.bn_stats(bst[:, c, j, :], src[:, c, j, :])
                    ins.then_inc(stats_local, 1)
                    dve.wait_ge(stats_local, 1)
                    dve.sem_clear(stats_local)
                    for j in range(NJ):
                        ins = v.bn_aggr(mv[:, c, j, :], bst[:, c, j, :])
                    ins.then_inc(stats_steps[c], 1)
                    dve.wait_ge(stats_steps[c], 6 * b + 2 * n + 1)
                    v.tensor_scalar(ve[:, c, :], mv[:, c, :, 1], EPS, None, ALU.add).then_inc(stats_steps[c], 1)
                if name == "norm":
                    c, n = args
                    src, dst = ((moe, moe), (attn, x1), (x2, x2))[n]
                    dve.wait_ge(rstd_ready[c], 3 * b + n + 1)
                    for j in range(NJ):
                        ins = v.tensor_scalar(dst[:, c, j, :], src[:, c, j, :], mv[:, c, j, 0:1],
                                              rstd[:, c, j:j + 1], ALU.subtract, ALU.mult)
                    ins.then_inc(normed[c], 1)
                if name == "x_low":
                    (c,) = args
                    dve.wait_ge(x_high[c], b + 1)
                    v.tensor_tensor(x1l[:, :], bank["T"][:, :], x1h[:, :].bitcast(F32), ALU.subtract
                                    ).then_inc(drained["T"], 1)
                if name == "ff_mul":
                    (c,) = args
                    for m in range(NH):
                        dve.wait_ge(drained["U0"], it.fills("U0", stage, ("ff_up", c), m))
                        dve.wait_ge(filled["U1"], it.fills("U1", stage, ("ff_up", c), m))
                        v.scalar_tensor_tensor(out=hh[:, m, :], in0=bank["U1"][:, :], scalar=INV127, in1=hh[:, m, :],
                                               op0=ALU.mult, op1=ALU.mult).then_inc(drained["U1"], 1)

            def body(it):
                b = it.b["A"]
                if it.runs["A"]:
                    dve.wait_ge(parts_ready, b + 1)
                    v.tensor_copy(bc_parts[:, :], parts[:, :]).then_inc(bc_parts_ready, 1)
                    wait(dve, decay_ready, S * b)
                    v.tensor_copy(delta[:, :], next_delta[:, :]).then_inc(delta_ready, 1)
                    v.tensor_tensor(dx[:, :], next_delta[:, :], xT_sb[:, :], ALU.mult).then_inc(dx_ready, 1)
                    clips = dve.value_load(clip_flag[0:1, 0:1], min_val=0, max_val=128)
                for s in range(S):
                    if it.runs["A"]:
                        if s == 0:
                            wait_apart(dve, dx_ready, b + 1)
                        with dve.If(clips > 0):
                            dve.wait_ge(b_ready, S * b + s + 1)
                            slow_input(b, s)
                            dve.wait_ge(decay_ready, S * b + s + 1)
                            dve.wait_ge(inp_ready, S * b + s + 1)
                            slow_scan(s)
                        with dve.Else():
                            dve.wait_ge(b_ready, S * b + s + 1)
                            fast_input(s)
                            dve.wait_ge(decay_ready, S * b + s + 1)
                            dve.wait_ge(inp_ready, S * b + s + 1)
                            v.tensor_tensor_scan(state[:, :], decay[:, s % NDECAY, :], inp[:, :], 0.0, ALU.mult,
                                                 ALU.add).then_inc(state_ready, 1)
                        dve.nop()
                    for t in it.tasks(DVE_STEPS, 2 * s):
                        run(it, *t)
                    if it.runs["A"]:
                        dve.wait_ge(c_ready, S * b + s + 1)
                        dve.wait_ge(state_ready, S * b + s + 1)
                        wait(dve, added, S * b + s - NPROD + 1)
                        v.tensor_tensor(prod[:, s % NPROD, :], state[:, :], psC[:, :], ALU.mult
                                        ).then_inc(prod_ready, 1)
                    for t in it.tasks(DVE_STEPS, 2 * s + 1):
                        run(it, *t)

            iterate(dve, body)

        @block.gpsimd
        def _(pool):
            g = nc.gpsimd

            def run(it, stage, name, *args):
                b = it.b[stage]
                if name == "bc_rest":
                    pool.wait_ge(parts_high, b + 1)
                    wait(pool, parts_ready, b)
                    g.tensor_tensor(rest[:, :], bcf[:, :], parts[:, :], ALU.subtract
                                    ).then_inc(rest_ready, 1)
                if name == "bound_input":
                    pool.wait_ge(x_scaled, 2 * b + 1)
                    for c in range(2):
                        pool.wait_ge(drained["T"], it.fills("T", "P", ("b_spread", c)))
                        g.tensor_tensor(half(bnd, c), half(bnd, c), half(x_abs, c), ALU.mult).then_inc(bnd_ready, 1)
                if name == "mix":
                    k = args[0]
                    c, e = divmod(k, E)
                    dst = moe[:, c, :, :].rearrange("p j d -> p (j d)")
                    pool.wait_ge(drained["D"], it.fills("D", "B", ("down", k)))
                    if e == 0:
                        wait(pool, affine_steps[c], 3 * b)
                        pool.wait_ge(drained["T"], it.fills("T", "B", ("y_turn",), c))
                    wait(pool, mixed, 8 * b + k)
                    g.tensor_tensor(dst, ytok[:, c, :] if e == 0 else dst,
                                    weighed[:, k % 2, :, :].rearrange("p j d -> p (j d)"), ALU.add
                                    ).then_inc(mixed, 1)
                if name == "rstd":
                    c, n = args
                    pool.wait_ge(stats_steps[c], 6 * b + 2 * n + 2)
                    wait(pool, normed[c], 3 * b + n)
                    g.tensor_tensor(rstd[:, c, :], ve[:, c, :], minus_half[:, :], ALU.pow).then_inc(rstd_ready[c], 1)
                if name == "affine":
                    (c,) = args
                    pool.wait_ge(normed[c], 3 * b + 1)
                    flat = moe[:, c, :, :]
                    lw = lnw_sb[:, :].rearrange("p (o d) -> p o d", o=1).to_broadcast([128, NJ, D])
                    lb = lnb_sb[:, :].rearrange("p (o d) -> p o d", o=1).to_broadcast([128, NJ, D])
                    g.tensor_tensor(flat, flat, lw, ALU.mult).then_inc(affine_steps[c], 1)
                    pool.wait_ge(affine_steps[c], 3 * b + 1)
                    g.tensor_tensor(flat, flat, lb, ALU.add).then_inc(affine_steps[c], 1)
                    pool.wait_ge(affine_steps[c], 3 * b + 2)
                    pool.wait_ge(xt_in[c], 16 * (b + 1))
                    wait(pool, normed[c], 3 * b - 1)
                    g.tensor_tensor(attn[:, c, :, :], flat, xt[:, c, :, :], ALU.add).then_inc(affine_steps[c], 1)

            def body(it):
                b = it.b["A"]
                for s in range(S):
                    for t in it.tasks(POOL_STEPS, 2 * s):
                        run(it, *t)
                    if it.runs["A"]:
                        pool.wait_ge(prod_ready, S * b + s + 1)
                        if s == 0:
                            pool.wait_ge(x_scaled, 2 * (b + 1))
                        wait(pool, added, S * b + s)
                        if s == S - 1 and it.runs["B"]:
                            pool.wait_ge(filled["U1"], it.fills("U1", "B", ("up", 7), 1))
                        g.tensor_tensor((y if s == S - 1 else yacc)[:, :], prod[:, s % NPROD, :],
                                        (xD if s == 0 else yacc)[:, :], ALU.add).then_inc(added, 1)
                    for t in it.tasks(POOL_STEPS, 2 * s + 1):
                        run(it, *t)

            pool.wait_ge(consts_in, 16 * 16)
            pool.wait_ge(consts_ready, 2)
            iterate(pool, body)


def kernel(**inputs):
    import concourse.bacc as bacc
    from concourse.bass_utils import run_bass_kernel_spmd

    a = {k[3:]: np.asarray(v) for k, v in inputs.items()}
    x = np.ascontiguousarray(a["attn_x"])
    wb, wc = a["attn_WB"], a["attn_WC"]
    none = np.zeros((D, 32), wb.dtype)
    pad = np.zeros(32, wb.dtype)
    bcb = np.concatenate([a["attn_bB"], a["attn_bC"]])
    sel = np.zeros((128, 2 * S), np.float32)
    for row in (0, 64, 96):
        sel[row:row + 2 * S] = np.eye(2 * S, dtype=np.float32)
    arrays = {
        "xT": x.transpose(0, 2, 1), "x": x, "a_log": a["attn_A_log"], "d_param": a["attn_D_param"].reshape(D, 1),
        "wd": a["attn_Wd"], "bd": a["attn_bd"].reshape(D, 1),
        "wbc": np.concatenate([wb, wc, none, wb, wc, wb, wc], axis=1),
        "bbc": np.concatenate([bcb, pad, bcb, bcb]).reshape(128, 1),
        "wr": a["attn_Wr"], "br": a["attn_br"].reshape(1, E), "up_w": a["attn_up_w"],
        "up_b": a["attn_up_b"].reshape(E * NF, 128).T, "down_w": a["attn_down_w"],
        "down_b": a["attn_down_b"].reshape(1, E * D), "ln_w": a["attn_ln_w"].reshape(1, D),
        "ln_b": a["attn_ln_b"].reshape(1, D), "wg": a["ffn_w_gate"].T, "wu": a["ffn_w_up"].T,
        "wdn": a["ffn_w_down"].T, "ident": np.eye(128, dtype=np.float32), "sel": sel,
        "rev": np.arange(E, 0, -1, dtype=np.float32).reshape(1, E),
    }
    nc = bacc.Bacc("TRN2", target_bir_lowering=False, num_devices=1)
    feed, args = {}, []
    for name, v in arrays.items():
        v = np.ascontiguousarray(v)
        feed[f"in_{name}"] = v
        args.append(nc.dram_tensor(f"in_{name}", v.shape, mybir.dt.from_np(v.dtype), kind="ExternalInput").ap())
    out = nc.dram_tensor("out", (NB, L, D), F32, kind="ExternalOutput").ap()
    ssm_moe_ffn_kernel(nc, *args, out)
    r = run_bass_kernel_spmd(nc, [feed], core_ids=[0])
    return r.results[0]["out"]
```

```python
from contextlib import ExitStack

import numpy as np

import concourse.bass as bass
from concourse import mybir

F32 = mybir.dt.float32
F32R = mybir.dt.float32r
BF16 = mybir.dt.bfloat16
I32 = mybir.dt.int32
ALU = mybir.AluOpType
ACT = mybir.ActivationFunctionType
X = mybir.AxisListType.X

NB, L, D = 8, 1024, 128
S = 16
E, F = 4, 512
NF = F // 128
H = 384
NH = H // 128
HALF = 512
NJ = HALF // 128
EPS = 1e-5
INV127 = 1.0 / 127.0
CLIP_B, CLIP_H = 2.0, 100.0
SAFE_B, SAFE_H = 1.98, 90.0
NDECAY = 8
NPROD = 4
FIRST_FULL, LAST_FULL = 3, 6

Y_GROUPS = [(0, 3), (3, 6), (6, 8)]
DE = D + E

PE_STEPS = [
    (0, 'C', 'ff_up', 0), (0, 'B', 'y_turn'), (2, 'B', 'up', 0), (3, 'C', 'ff_down', 0),
    (4, 'B', 'up', 1), (4, 'B', 'down', 0), (6, 'B', 'down', 1), (7, 'B', 'up', 2),
    (9, 'B', 'up', 3), (10, 'P', 'z'), (11, 'P', 'bc'), (11, 'B', 'down', 2),
    (13, 'B', 'down', 3), (14, 'P', 'b_turn'), (15, 'C', 'x_turn', 1), (16, 'B', 'up', 4),
    (17, 'B', 'up', 5), (18, 'C', 'ff_up', 1), (19, 'B', 'down', 4), (20, 'B', 'down', 5),
    (22, 'C', 'ff_down', 1), (23, 'B', 'up', 6), (24, 'P', 'b_spread', 0), (24, 'B', 'up', 7),
    (25, 'P', 'b_spread', 1), (26, 'B', 'down', 6), (29, 'B', 'down', 7), (30, 'P', 'flag'),
    (30, 'B', 'x_turn', 0),
]
ACT_STEPS = [
    (0, 'C', 'gate', 0), (1, 'B', 'y_copy'), (2, 'B', 'silu', 0), (3, 'B', 'silu', 1),
    (4, 'B', 'router_exp'), (4, 'A', 'decay', 4, 9), (8, 'B', 'silu', 2), (9, 'B', 'silu', 3),
    (10, 'P', 'z_copy'), (11, 'A', 'decay', 9, 12), (12, 'P', 'bc_copy'), (12, 'P', 'softplus'),
    (14, 'P', 'bc_mid'), (15, 'C', 'x_high', 1), (16, 'B', 'silu', 4), (17, 'B', 'silu', 5),
    (18, 'C', 'gate', 1), (19, 'A', 'decay', 12, 16), (23, 'B', 'silu', 6), (24, 'B', 'silu', 7),
    (24, 'P', 'x_scaled'), (25, 'P', 'decay_bound'), (25, 'P', 'decay', 0, 4),
    (30, 'B', 'x_high', 0),
]
DVE_STEPS = [
    (0, 'C', 'ff_mul', 0), (2, 'B', 'router_shift'), (2, 'C', 'stats', 1, 0),
    (4, 'C', 'norm', 1, 0), (4, 'C', 'ff_sum', 0), (5, 'B', 'router_pick'), (5, 'B', 'weigh', 0),
    (7, 'B', 'weigh', 1), (8, 'C', 'stats', 1, 1), (9, 'C', 'norm', 0, 2),
    (11, 'C', 'norm', 1, 1), (14, 'B', 'weigh', 2), (14, 'B', 'weigh', 3), (15, 'P', 'b_max'),
    (16, 'B', 'stats', 0, 0), (16, 'C', 'x_low', 1), (17, 'P', 'bc_low'), (19, 'B', 'norm', 0, 0),
    (19, 'C', 'ff_mul', 1), (20, 'P', 'delta'), (20, 'B', 'weigh', 4), (21, 'B', 'stats', 0, 1),
    (21, 'B', 'weigh', 5), (22, 'C', 'ff_sum', 1), (24, 'P', 'bound', 0), (24, 'C', 'norm', 1, 2),
    (26, 'P', 'bound', 1), (26, 'B', 'norm', 0, 1), (28, 'B', 'weigh', 6), (28, 'P', 'majorant'),
    (30, 'B', 'weigh', 7), (30, 'P', 'flag'), (31, 'B', 'x_low', 0),
]
POOL_STEPS = [
    (2, 'C', 'rstd', 1, 0), (5, 'C', 'affine', 1), (5, 'C', 'rstd', 0, 2), (7, 'B', 'mix', 0),
    (7, 'B', 'mix', 1), (10, 'C', 'rstd', 1, 1), (12, 'P', 'bc_rest'), (14, 'B', 'mix', 2),
    (14, 'B', 'mix', 3), (17, 'B', 'rstd', 0, 0), (19, 'B', 'affine', 0), (21, 'C', 'rstd', 1, 2),
    (21, 'B', 'mix', 4), (23, 'B', 'mix', 5), (24, 'B', 'rstd', 0, 1), (25, 'P', 'bound_input'),
    (28, 'B', 'mix', 6), (30, 'B', 'mix', 7),
]


def banks_of(task):
    name = task[0]
    if name in ("z", "bc"):
        return ["U0", "U1"]
    if name == "up":
        return ["U0", "U1"] * (NF // 2)
    if name == "ff_up":
        return ["U0", "U1"] * NH
    if name == "y_turn":
        return ["T", "D", "T"]
    if name == "down":
        return ["T"] if task[1] in (0, 3, 5) else ["D"]
    return ["D"] if name == "ff_down" else ["T"]


class Iteration:

    def __init__(self, i):
        full = not isinstance(i, int)
        offset = {"P": 1, "A": 0, "B": -1, "C": -2}
        self.b, self.runs, self.ran = {}, {}, {}
        for stage, d in offset.items():
            self.b[stage] = i + d
            self.runs[stage] = full or 0 <= i + d < NB
            self.ran[stage] = i + d if full else min(max(i + d, 0), NB)

    def tasks(self, steps, step):
        return [t[1:] for t in steps if t[0] == step and self.runs[t[1]]]

    def fills(self, bank, stage=None, task=(), k=0):
        before, count = 0, None
        per = {"P": 0, "B": 0, "C": 0}
        for t in PE_STEPS:
            n = sum(x == bank for x in banks_of(t[2:]))
            per[t[1]] += n
            if t[1:] == (stage, *task):
                count = before + k + 1
            if self.runs[t[1]]:
                before += n
        assert count is not None or stage is None
        return sum(per[s] * self.ran[s] for s in per) + (count or 0)


def ssm_moe_ffn_kernel(nc, xT, x, a_log, d_param, wd, bd, wbc, bbc, wr, br, up_w, up_b, down_w, down_b,
                       ln_w, ln_b, wg, wu, wdn, ident_c, sel_c, rev_c, out):
    ctx = ExitStack()
    with ctx:
        def sb(name, shape, dt=F32):
            return ctx.enter_context(nc.sbuf_tensor(name, shape, dt))

        def pb(name, shape, dt=F32):
            return ctx.enter_context(nc.psum_tensor(name, shape, dt))

        def sem(name):
            return ctx.enter_context(nc.semaphore(name))

        wd_sb = sb("wd_sb", [D, D])
        wbc_sb = sb("wbc_sb", [D, 128])
        up_sb = sb("up_sb", [D, E, F])
        down_sb = sb("down_sb", [128, E * NF, D])
        wg_sb = sb("wg_sb", [D, H], F32R)
        wu_sb = sb("wu_sb", [D, H], F32R)
        wdn_sb = sb("wdn_sb", [128, NH, D])
        a_sb = sb("a_sb", [D, S])
        a_max = sb("a_max", [D, 1])
        dpar = sb("dpar", [D, 1])
        bd_sb = sb("bd_sb", [D, 1])
        bbc_sb = sb("bbc_sb", [128, 1])
        upb_sb = sb("upb_sb", [128, E * NF])
        br_sb = sb("br_sb", [128, E])
        rev_sb = sb("rev_sb", [128, E])
        lnw_sb = sb("lnw_sb", [128, D])
        lnb_sb = sb("lnb_sb", [128, D])
        ident_wr = sb("ident_wr", [128, DE])
        ident = ident_wr[:, 0:D]
        identb = sb("identb", [128, 128], BF16)
        selcol = sb("selcol", [128, 2 * S])
        sel = sb("sel", [128, 2 * S, 128], BF16)
        bias_down = sb("bias_down", [128, E, NJ, D], BF16)
        ones_col = sb("ones_col", [128, 1])
        minus_half = sb("minus_half", [128, NJ])
        limits = sb("limits", [128, 3])
        xT_sb = sb("xT_sb", [D, L])
        zb = sb("zb", [D, L])
        sp = sb("sp", [D, L])
        bcf = sb("bcf", [128, L])
        rest = sb("rest", [128, L])
        parts = sb("parts", [128, L], BF16)
        bmax = sb("bmax", [128, 2 * NJ], BF16)
        next_delta = sb("next_delta", [D, L])
        amx = sp
        x_abs = zb
        bnd = sb("bnd", [D, L])
        xD = sb("xD", [D, L])
        peak = sb("peak", [D, 3])
        over = sb("over", [D, 3])
        holder = sb("holder", [128, 1])
        clip_flag = sb("clip_flag", [1, 1], I32)
        bc_parts = sb("bc_parts", [128, L], BF16)
        delta = sb("delta", [D, L])
        dx = sb("dx", [D, L])
        x_again = sb("x_again", [D, L])
        decay = sb("decay", [D, NDECAY, L])
        inp = sb("inp", [D, L])
        state = sb("state", [D, L])
        prod = sb("prod", [D, NPROD, L])
        yacc = sb("yacc", [D, L])
        y = sb("y", [D, L])
        xt = sb("xt", [128, 2, NJ, D])
        ytok = sb("ytok", [128, 2 * NJ, DE])
        rs = sb("rs", [128, 2 * NJ, E])
        ex = sb("ex", [128, 2 * NJ, E])
        rsmall = sb("rsmall", [128, 4, 2 * NJ])
        rcode = sb("rcode", [128, 2 * NJ, E])
        top_w = sb("top_w", [128, 2 * NJ, E])
        hid = sb("hid", [128, 2, NF, HALF])
        weighed = sb("weighed", [128, 2, NJ, D])
        moe = sb("moe", [128, 2, NJ, D])
        attn = sb("attn", [128, 2, NJ, D])
        x1 = sb("x1", [128, 2, NJ, D])
        x1h = sb("x1h", [D, HALF], F32R)
        x1l = sb("x1l", [D, HALF], F32R)
        hh = sb("hh", [128, NH, HALF])
        x2 = sb("x2", [128, 2, NJ, D])
        bst = sb("bst", [128, 2, NJ, 6])
        mv = sb("mv", [128, 2, NJ, 2])
        ve = sb("ve", [128, 2, NJ])
        rstd = sb("rstd", [128, 2, NJ])

        psB = pb("psB", [D, L])
        psC = pb("psC", [D, L])
        bank = {n: pb("ps" + n, [128, HALF]) for n in ("U0", "U1", "D", "T")}
        filled = {n: sem(f"filled_{n}") for n in bank}
        drained = {n: sem(f"drained_{n}") for n in bank}

        consts_in = sem("consts_in")
        bias_rows_in = sem("bias_rows_in")
        ff_in = sem("ff_in")
        setup_dve = sem("setup_dve")
        setup_act = sem("setup_act")
        consts_ready = sem("consts_ready")
        xT_in = sem("xT_in")
        x_again_in = sem("x_again_in")
        xt_in = [sem(f"xt_in{c}") for c in range(2)]
        out_done = [sem(f"out_done{c}") for c in range(2)]
        parts_high = sem("parts_high")
        rest_ready = sem("rest_ready")
        parts_mid = sem("parts_mid")
        parts_ready = sem("parts_ready")
        softplus_steps = sem("softplus_steps")
        delta_next = sem("delta_next")
        x_scaled = sem("x_scaled")
        amx_ready = sem("amx_ready")
        bnd_ready = sem("bnd_ready")
        flag_steps = sem("flag_steps")
        bc_parts_ready = sem("bc_parts_ready")
        dx_ready = sem("dx_ready")
        b_ready = sem("b_ready")
        c_ready = sem("c_ready")
        decay_ready = sem("decay_ready")
        inp_ready = sem("inp_ready")
        state_ready = sem("state_ready")
        prod_ready = sem("prod_ready")
        added = sem("added")
        slow_steps = sem("slow_steps")
        stats_local = sem("stats_local")
        router_steps = sem("router_steps")
        router_exp = sem("router_exp")
        mixed = sem("mixed")
        stats_steps = [sem(f"stats_steps{c}") for c in range(2)]
        rstd_ready = [sem(f"rstd_ready{c}") for c in range(2)]
        normed = [sem(f"normed{c}") for c in range(2)]
        affine_steps = [sem(f"affine_steps{c}") for c in range(2)]
        x_high = [sem(f"x_high{c}") for c in range(2)]

        def wait(eng, s, value):
            if not isinstance(value, int) or value > 0:
                eng.wait_ge(s, value)

        def iterate(eng, body):
            for i in range(-1, FIRST_FULL):
                body(Iteration(i))
            with eng.Fori(FIRST_FULL, LAST_FULL + 1) as i:
                body(Iteration(i))
            for i in range(LAST_FULL + 1, NB + 2):
                body(Iteration(i))

        def half(t, c):
            return t[:, c * HALF:(c + 1) * HALF]

        def by_token(n):
            return bank[n][:, :].rearrange("p (j d) -> p j d", j=NJ)

        block = ctx.enter_context(nc.Block())

        @block.sync
        def _(sp_):
            for dst, src in (
                (wd_sb[:, :], wd), (wbc_sb[:, :], wbc), (bd_sb[:, :], bd), (bbc_sb[:, :], bbc),
                (a_sb[:, :], a_log), (dpar[:, :], d_param), (ident_wr[:, D:DE], wr), (ident, ident_c),
                (selcol[:, :], sel_c), (rev_sb[:, :], rev_c.to_broadcast([128, E])),
                (br_sb[:, :], br.to_broadcast([128, E])),
                (lnw_sb[:, :], ln_w.to_broadcast([128, D])), (lnb_sb[:, :], ln_b.to_broadcast([128, D])),
                (upb_sb[:, :], up_b), (up_sb[:, :, :], up_w.rearrange("e d f -> d e f")),
                (down_sb[:, :, :], down_w.rearrange("e (n p) d -> p (e n) d", p=128)),
            ):
                sp_.dma_start(dst, src).then_inc(consts_in, 16)
            stage = hid[:, 0, :, :].rearrange("p n t -> p (n t)").bitcast(I32)
            for k, w in enumerate((wg, wu, wdn)):
                dst = stage[:, k * H:(k + 1) * H]
                if k == 2:
                    dst = dst.rearrange("p (m d) -> p m d", m=NH)
                    w = w.rearrange("(m p) d -> p m d", p=128)
                sp_.dma_start(dst, w).then_inc(ff_in, 16)
            sp_.wait_ge(setup_dve, 1)
            for row in (0, 64, 96):
                sp_.dma_start(rest[row:row + 1, 0:E * D], down_b).then_inc(bias_rows_in, 16)

            def body(it):
                if it.runs["P"]:
                    b = it.b["P"]
                    wait(sp_, x_scaled, 2 * b)
                    wait(sp_, dx_ready, b)
                    sp_.dma_start(xT_sb[:, :], xT[b]).then_inc(xT_in, 16)
                if it.runs["A"]:
                    b = it.b["A"]
                    wait(sp_, prod_ready, S * b)
                    wait(sp_, x_again_in, 16 * b)
                    sp_.dma_start(x_again[:, :], xT[b]).then_inc(x_again_in, 16)
                if it.runs["B"]:
                    b = it.b["B"]
                    for c in range(2):
                        wait(sp_, affine_steps[c], 3 * b)
                        sp_.dma_start(xt[:, c, :, :], x[b].rearrange("(c j p) d -> c p j d", p=128, c=2)[c]
                                      ).then_inc(xt_in[c], 16)
                if it.runs["C"]:
                    b = it.b["C"]
                    for c in range(2):
                        wait(sp_, normed[c], 3 * b + 3)
                        sp_.dma_start(out[b].rearrange("(c j p) d -> c p j d", p=128, c=2)[c], x2[:, c, :, :]
                                      ).then_inc(out_done[c], 16)

            iterate(sp_, body)
            for c in range(2):
                sp_.wait_ge(out_done[c], 16 * NB)
            sp_.wait_ge(x_again_in, 16 * NB)

        @block.tensor
        def _(pe):
            def scan_operand(it, s, which):
                b = it.b["A"]
                ps, ready, used = (psB, b_ready, inp_ready) if which == 0 else (psC, c_ready, prod_ready)
                wait(pe, used, S * b + s)
                if which == 0 and s == 0:
                    wait(pe, bc_parts_ready, b + 1)
                for c in range(2):
                    mm = pe.matmul(half(ps, c), sel[:, which * S + s, :], half(bc_parts, c), start=True, stop=True)
                mm.then_inc(ready, 1)

            def fill(it, name, stage, task, k=0):
                wait(pe, drained[name], it.fills(name, stage, task, k) - 1)

            def run(it, stage, name, *args):
                b = it.b[stage]
                task = (name, *args)
                banks = banks_of(task)
                if name in ("z", "bc"):
                    wait(pe, xT_in, 16 * (b + 1))
                    for c in range(2):
                        fill(it, banks[c], stage, task)
                        pe.matmul(bank[banks[c]][:, :], (wd_sb if name == "z" else wbc_sb)[:, :], half(xT_sb, c),
                                  start=True, stop=True).then_inc(filled[banks[c]], 1)
                if name == "b_turn":
                    wait(pe, drained["U1"], it.fills("U1", "P", ("bc",)))
                    fill(it, "T", stage, task)
                    pe.matmul(bank["T"][:, 0:1], identb[:, :], identb[:, 0:1], start=True, stop=True)
                    for j in range(2 * NJ):
                        mm = pe.transpose(bank["T"][:, j * 32:j * 32 + 32], bcf[0:32, j * 128:(j + 1) * 128],
                                          ident[0:32, 0:32])
                    mm.then_inc(filled["T"], 1)
                if name == "b_spread":
                    (c,) = args
                    wait(pe, drained["T"], it.fills("T", "P", ("b_turn",)))
                    fill(it, "T", stage, task)
                    for j in range(NJ):
                        mm = pe.matmul(bank["T"][:, j * 128:(j + 1) * 128],
                                       bmax[:, c * NJ + j:c * NJ + j + 1].to_broadcast([128, 128]), identb[:, :],
                                       start=True, stop=True)
                    mm.then_inc(filled["T"], 1)
                if name == "flag":
                    wait(pe, flag_steps, 3 * b + 3)
                    fill(it, "T", stage, task)
                    pe.matmul(bank["T"][0:1, 0:3], ones_col[:, :], over[:, :], start=True, stop=True
                              ).then_inc(filled["T"], 1)
                if name == "y_turn":
                    wait(pe, added, S * (b + 1))
                    for n, (j0, j1) in enumerate(Y_GROUPS):
                        t = banks[n]
                        fill(it, t, stage, task, n // 2)
                        for j in range(j0, j1):
                            mm = pe.matmul(bank[t][:, (j - j0) * DE:(j - j0 + 1) * DE],
                                           y[:, j * 128:(j + 1) * 128], ident_wr[:, :], start=True, stop=True)
                        mm.then_inc(filled[t], 1)
                if name == "up":
                    c, e = divmod(args[0], E)
                    for f in range(NF):
                        fill(it, banks[f], stage, task, f // 2)
                        pe.matmul(bank[banks[f]][:, :], up_sb[:, e, f * 128:(f + 1) * 128], half(y, c),
                                  start=True, stop=True).then_inc(filled[banks[f]], 1)
                if name == "down":
                    k = args[0]
                    e = k % E
                    d = banks[0]
                    fill(it, d, stage, task)
                    pe.matmul(bank[d][:, :], sel[:, 0, :],
                              bias_down[:, e, :, :].rearrange("p j d -> p (j d)"), start=True, stop=False,
                              skip_group_check=True)
                    for u in ("U0", "U1"):
                        wait(pe, drained[u], it.fills(u, "B", ("up", k), 1))
                    for j in range(NJ):
                        for f in range(NF):
                            mm = pe.matmul(bank[d][:, j * 128:(j + 1) * 128],
                                           hid[:, k % 2, f, j * 128:(j + 1) * 128], down_sb[:, e * NF + f, :],
                                           start=False, stop=(f == NF - 1), skip_group_check=True)
                    mm.then_inc(filled[d], 1)
                if name == "x_turn":
                    (c,) = args
                    wait(pe, normed[c], 3 * b + 2)
                    fill(it, "T", stage, task)
                    for j in range(NJ):
                        mm = pe.transpose(bank["T"][:, j * 128:(j + 1) * 128], x1[:, c, j, :], ident)
                    mm.then_inc(filled["T"], 1)
                if name == "ff_up":
                    (c,) = args
                    wait(pe, drained["T"], it.fills("T", stage, ("x_turn", c)) if c else it.fills("T"))
                    for n in range(2 * NH):
                        w, m = (wg_sb, wu_sb)[n // NH], n % NH
                        u = banks[n]
                        fill(it, u, stage, task, n // 2)
                        pe.matmul(bank[u][:, :], w[:, m * 128:(m + 1) * 128], x1h[:, :], start=True, stop=False)
                        pe.matmul(bank[u][:, :], w[:, m * 128:(m + 1) * 128], x1l[:, :], start=False, stop=True
                                  ).then_inc(filled[u], 1)
                if name == "ff_down":
                    (c,) = args
                    wait(pe, drained["U1"], it.fills("U1", stage, ("ff_up", c), NH - 1))
                    fill(it, "D", stage, task)
                    for j in range(NJ):
                        for m in range(NH):
                            mm = pe.matmul(bank["D"][:, j * 128:(j + 1) * 128], hh[:, m, j * 128:(j + 1) * 128],
                                           wdn_sb[:, m, :], start=(m == 0), stop=(m == NH - 1),
                                           skip_group_check=True)
                    mm.then_inc(filled["D"], 1)

            def body(it):
                for s in range(S):
                    if it.runs["A"]:
                        if s == 0:
                            scan_operand(it, 0, 0)
                        scan_operand(it, s, 1)
                    for t in it.tasks(PE_STEPS, 2 * s):
                        run(it, *t)
                    if it.runs["A"] and s + 1 < S:
                        scan_operand(it, s + 1, 0)
                    for t in it.tasks(PE_STEPS, 2 * s + 1):
                        run(it, *t)

            pe.wait_ge(consts_in, 16 * 16)
            pe.wait_ge(consts_ready, 2)
            iterate(pe, body)

        @block.scalar
        def _(act):
            act.wait_ge(consts_in, 16 * 16)
            nc.scalar.activation(a_sb[:, :], a_sb[:, :], ACT.Exp).then_inc(setup_act, 1)
            act.wait_ge(setup_act, 1)
            nc.scalar.activation(a_sb[:, :], a_sb[:, :], ACT.Copy, scale=-1.0).then_inc(consts_ready, 1)
            act.wait_ge(consts_ready, 2)

            def run(it, stage, name, *args):
                b = it.b[stage]
                if name == "z_copy":
                    wait(act, bnd_ready, 2 * b)
                    for c, u in enumerate(("U0", "U1")):
                        act.wait_ge(filled[u], it.fills(u, "P", ("z",)))
                        nc.scalar.activation(half(zb, c), bank[u][:, :], ACT.Identity, bias=bd_sb[:, 0:1]
                                             ).then_inc(drained[u], 1)
                if name == "bc_copy":
                    wait(act, parts_ready, b)
                    wait(act, delta_next, b)
                    for c, u in enumerate(("U0", "U1")):
                        act.wait_ge(filled[u], it.fills(u, "P", ("bc",)))
                        nc.scalar.activation(half(bcf, c), bank[u][:, :], ACT.Identity, bias=bbc_sb[:, 0:1]
                                             ).then_inc(drained[u], 1)
                    wait(act, bc_parts_ready, b)
                    for u in ("U0", "U1"):
                        act.wait_ge(drained[u], it.fills(u, "P", ("bc",)))
                    nc.scalar.activation(parts[:, :], bcf[:, :], ACT.Copy).then_inc(parts_high, 1)
                if name == "bc_mid":
                    act.wait_ge(rest_ready, b + 1)
                    nc.scalar.activation(parts[64:128, :], rest[64:128, :], ACT.Copy).then_inc(parts_mid, 1)
                if name == "softplus":
                    wait(act, flag_steps, 3 * b)
                    for u in ("U0", "U1"):
                        act.wait_ge(drained[u], it.fills(u, "P", ("z",)))
                    nc.scalar.activation(sp[:, :], zb[:, :], ACT.Abs).then_inc(softplus_steps, 1)
                    act.wait_ge(softplus_steps, 3 * b + 1)
                    nc.scalar.activation(sp[:, :], sp[:, :], ACT.Exp, scale=-1.0).then_inc(softplus_steps, 1)
                    act.wait_ge(softplus_steps, 3 * b + 2)
                    nc.scalar.activation(sp[:, :], sp[:, :], ACT.Ln, bias=1.0).then_inc(softplus_steps, 1)
                if name == "x_scaled":
                    act.wait_ge(xT_in, 16 * (b + 1))
                    act.wait_ge(delta_next, b + 1)
                    nc.scalar.activation(x_abs[:, :], xT_sb[:, :], ACT.Abs).then_inc(x_scaled, 1)
                    wait(act, added, S * (b - 1) + 1)
                    nc.scalar.activation(xD[:, :], xT_sb[:, :], ACT.Copy, scale=dpar[:, 0:1]).then_inc(x_scaled, 1)
                if name == "decay_bound":
                    act.wait_ge(delta_next, b + 1)
                    nc.scalar.activation(amx[:, :], next_delta[:, :], ACT.Exp, scale=a_max[:, 0:1]
                                         ).then_inc(amx_ready, 1)
                if name == "decay":
                    for s in range(*args):
                        if s == 0:
                            act.wait_ge(delta_next, b + 1)
                        wait(act, state_ready, S * b + s - NDECAY + 1)
                        nc.scalar.activation(decay[:, s % NDECAY, :], next_delta[:, :], ACT.Exp, scale=a_sb[:, s:s + 1]
                                             ).then_inc(decay_ready, 1)
                if name == "y_copy":
                    wait(act, mixed, 8 * b)
                    for n, (j0, j1) in enumerate(Y_GROUPS):
                        t = banks_of(("y_turn",))[n]
                        act.wait_ge(filled[t], it.fills(t, "B", ("y_turn",), n // 2))
                        nc.scalar.activation(ytok[:, j0:j1, :].rearrange("p j d -> p (j d)"),
                                             bank[t][:, 0:(j1 - j0) * DE], ACT.Copy).then_inc(drained[t], 1)
                if name == "router_exp":
                    act.wait_ge(router_steps, 9 * b + 3)
                    nc.scalar.activation(ex[:, :, :], rs[:, :, :], ACT.Exp).then_inc(router_exp, 1)
                if name == "silu":
                    k = args[0]
                    for f in range(NF):
                        u = banks_of(("up", k))[f]
                        act.wait_ge(filled[u], it.fills(u, "B", ("up", k), f // 2))
                        nc.scalar.activation(hid[:, k % 2, f, :], bank[u][:, :], ACT.Silu,
                                             bias=upb_sb[:, (k % E) * NF + f:(k % E) * NF + f + 1]
                                             ).then_inc(drained[u], 1)
                if name == "x_high":
                    (c,) = args
                    act.wait_ge(filled["T"], it.fills("T", stage, ("x_turn", c)))
                    nc.scalar.activation(x1h[:, :], bank["T"][:, :], ACT.Copy).then_inc(x_high[c], 1)
                if name == "gate":
                    (c,) = args
                    for m in range(NH):
                        u, nth = f"U{m % 2}", m // 2
                        act.wait_ge(filled[u], it.fills(u, stage, ("ff_up", c), nth))
                        nc.scalar.activation(hh[:, m, :], bank[u][:, :], ACT.Silu, scale=INV127
                                             ).then_inc(drained[u], 1)

            def body(it):
                for step in range(2 * S):
                    for t in it.tasks(ACT_STEPS, step):
                        run(it, *t)

            iterate(act, body)

        @block.vector
        def _(dve):
            v = nc.vector
            steps = [0]

            def setup(ins):
                steps[0] += 1
                ins.then_inc(setup_dve, 1)
                dve.wait_ge(setup_dve, steps[0])

            setup(v.memset(rest[:, 0:E * D], 0.0))
            setup(v.memset(ones_col[:, :], 1.0))
            setup(v.memset(minus_half[:, :], -0.5))
            setup(v.memset(limits[:, 0:2], SAFE_B))
            setup(v.memset(limits[:, 2:3], SAFE_H))
            dve.wait_ge(consts_in, 16 * 16)
            setup(v.tensor_copy(identb[:, :], ident))
            setup(v.tensor_copy(sel[:, :, :], selcol[:, :].rearrange("p (s o) -> p s o", o=1).to_broadcast([128, 2 * S, 128])))
            dve.wait_ge(ff_in, 48)
            stage = hid[:, 0, :, :].rearrange("p n t -> p (n t)").bitcast(I32)
            setup(v.tensor_copy(wg_sb[:, :], stage[:, 0:H]))
            setup(v.tensor_copy(wu_sb[:, :], stage[:, H:2 * H]))
            setup(v.tensor_copy(wdn_sb[:, :, :].rearrange("p m d -> p (m d)"), stage[:, 2 * H:3 * H]))
            dve.wait_ge(bias_rows_in, 48)
            row = rest[:, 0:E * D]
            part = inp[:, 0:E * D // 2].bitcast(BF16)
            setup(v.tensor_copy(part, row))
            setup(v.tensor_tensor(row[64:128, :], row[64:128, :], part[64:128, :], ALU.subtract))
            setup(v.tensor_copy(part[64:128, :], row[64:128, :]))
            setup(v.tensor_tensor(part[96:128, :], row[96:128, :], part[96:128, :], ALU.subtract))
            for j in range(NJ):
                setup(v.tensor_copy(bias_down[:, :, j, :], part.rearrange("p (e d) -> p e d", e=E)))
            dve.wait_ge(consts_ready, 1)
            setup(v.tensor_reduce(a_max[:, :], a_sb[:, :], X, ALU.max))
            v.memset(peak[:, :], 0.0).then_inc(consts_ready, 1)
            dve.wait_ge(consts_ready, 2)

            def wide(t, n, d):
                return t.rearrange("p (n o) -> p n o", o=1).to_broadcast([128, n, d])

            def fast_input(s):
                v.tensor_tensor(inp[:, :], dx[:, :], psB[:, :], ALU.mult).then_inc(inp_ready, 1)

            def slow_input(b, s):
                dve.wait_ge(x_again_in, 16 * (b + 1))
                v.tensor_tensor(inp[:, :], delta[:, :], psB[:, :], ALU.mult).then_inc(slow_steps, 1)
                dve.wait_ge(slow_steps, 1)
                v.tensor_scalar(inp[:, :], inp[:, :], CLIP_B, -CLIP_B, ALU.min, ALU.max).then_inc(slow_steps, 1)
                dve.wait_ge(slow_steps, 2)
                dve.sem_clear(slow_steps)
                v.tensor_tensor(inp[:, :], inp[:, :], x_again[:, :], ALU.mult).then_inc(inp_ready, 1)

            def slow_scan(s):
                a = decay[:, s % NDECAY, :]

                def step(now, before):
                    if before is None:
                        v.tensor_copy(state[:, now], inp[:, now]).then_inc(slow_steps, 1)
                    else:
                        v.scalar_tensor_tensor(out=state[:, now], in0=a[:, now], scalar=state[:, before],
                                               in1=inp[:, now], op0=ALU.mult, op1=ALU.add).then_inc(slow_steps, 1)
                    dve.wait_ge(slow_steps, 1)
                    v.tensor_scalar(state[:, now], state[:, now], CLIP_H, -CLIP_H, ALU.min, ALU.max
                                    ).then_inc(slow_steps, 1)
                    dve.wait_ge(slow_steps, 2)
                    dve.sem_clear(slow_steps)

                step(slice(0, 1), None)
                with dve.Fori(1, L) as t:
                    step(bass.ds(t, 1), bass.ds(t - 1, 1))
                v.tensor_copy(state[:, L - 1:L], state[:, L - 1:L]).then_inc(state_ready, 1)

            def run(it, stage, name, *args):
                b = it.b[stage]
                if name == "b_max":
                    dve.wait_ge(filled["T"], it.fills("T", "P", ("b_turn",)))
                    v.tensor_reduce(bmax[:, :], bank["T"][:, 0:64 * NJ].rearrange("p (j s) -> p j s", s=32)[:, :, 0:S],
                                    X, ALU.max, apply_absolute_value=True).then_inc(drained["T"], 1)
                if name == "delta":
                    dve.wait_ge(softplus_steps, 3 * (b + 1))
                    wait(dve, decay_ready, S * b)
                    v.scalar_tensor_tensor(out=next_delta[:, :], in0=zb[:, :], scalar=0.0, in1=sp[:, :],
                                           op0=ALU.max, op1=ALU.add).then_inc(delta_next, 1)
                if name == "bc_low":
                    dve.wait_ge(parts_mid, b + 1)
                    v.tensor_tensor(parts[96:128, :], rest[96:128, :], parts[96:128, :], ALU.subtract
                                    ).then_inc(parts_ready, 1)
                if name == "bound":
                    (c,) = args
                    dve.wait_ge(delta_next, b + 1)
                    dve.wait_ge(filled["T"], it.fills("T", "P", ("b_spread", c)))
                    v.memset(holder[:, :], 0.0)
                    v.tensor_tensor_reduce(half(bnd, c), half(next_delta, c), bank["T"][:, :], 1.0, 0.0,
                                           ALU.mult, ALU.max, peak[:, c:c + 1]).then_inc(drained["T"], 1)
                if name == "majorant":
                    dve.wait_ge(amx_ready, b + 1)
                    dve.wait_ge(bnd_ready, 2 * (b + 1))
                    wait(dve, state_ready, S * b - 1)
                    v.tensor_tensor_scan(inp[:, :], amx[:, :], bnd[:, :], 0.0, ALU.mult, ALU.add
                                         ).then_inc(flag_steps, 1)
                    dve.wait_ge(flag_steps, 3 * b + 1)
                    v.tensor_reduce(peak[:, 2:3], inp[:, :], X, ALU.max).then_inc(flag_steps, 1)
                    dve.wait_ge(flag_steps, 3 * b + 2)
                    dve.wait_ge(drained["T"], it.fills("T", "P", ("b_spread", 1)))
                    v.tensor_tensor(over[:, :], peak[:, :], limits[:, :], ALU.is_gt).then_inc(flag_steps, 1)
                if name == "flag":
                    dve.wait_ge(filled["T"], it.fills("T", "P", ("flag",)))
                    v.tensor_reduce(clip_flag[:, :], bank["T"][0:1, 0:3], X, ALU.max).then_inc(drained["T"], 1)
                    dve.wait_ge(drained["T"], it.fills("T", "P", ("flag",)))
                if name == "router_shift":
                    dve.wait_ge(drained["T"], it.fills("T", "B", ("y_turn",), 1))
                    v.tensor_tensor(rs[:, :, :], ytok[:, :, D:DE],
                                    br_sb[:, :].rearrange("p (o e) -> p o e", o=1).to_broadcast([128, 2 * NJ, E]),
                                    ALU.add).then_inc(router_steps, 1)
                    dve.wait_ge(router_steps, 9 * b + 1)
                    v.tensor_reduce(rsmall[:, 0, :], rs[:, :, :], X, ALU.max).then_inc(router_steps, 1)
                    dve.wait_ge(router_steps, 9 * b + 2)
                    v.tensor_tensor(rs[:, :, :], rs[:, :, :], wide(rsmall[:, 0, :], 2 * NJ, E), ALU.subtract
                                    ).then_inc(router_steps, 1)
                    dve.wait_ge(router_steps, 9 * b + 3)
                    v.scalar_tensor_tensor(out=rcode[:, :, :], in0=rs[:, :, :], scalar=0.0,
                                           in1=rev_sb[:, :].rearrange("p (o e) -> p o e", o=1).to_broadcast([128, 2 * NJ, E]),
                                           op0=ALU.is_equal, op1=ALU.mult).then_inc(router_steps, 1)
                if name == "router_pick":
                    dve.wait_ge(router_steps, 9 * b + 4)
                    v.tensor_reduce(rsmall[:, 1, :], rcode[:, :, :], X, ALU.max).then_inc(router_steps, 1)
                    dve.wait_ge(router_exp, b + 1)
                    v.tensor_reduce(rsmall[:, 2, :], ex[:, :, :], X, ALU.add).then_inc(router_steps, 1)
                    dve.wait_ge(router_steps, 9 * b + 6)
                    v.reciprocal(rsmall[:, 3, :], rsmall[:, 2, :]).then_inc(router_steps, 1)
                    v.tensor_tensor(top_w[:, :, :], rcode[:, :, :], wide(rsmall[:, 1, :], 2 * NJ, E), ALU.is_equal
                                    ).then_inc(router_steps, 1)
                    dve.wait_ge(router_steps, 9 * b + 8)
                    v.tensor_tensor(top_w[:, :, :], top_w[:, :, :], wide(rsmall[:, 3, :], 2 * NJ, E), ALU.mult
                                    ).then_inc(router_steps, 1)
                if name == "weigh":
                    k = args[0]
                    c, e = divmod(k, E)
                    (d,) = banks_of(("down", k))
                    dve.wait_ge(filled[d], it.fills(d, "B", ("down", k)))
                    dve.wait_ge(router_steps, 9 * (b + 1))
                    wait(dve, mixed, 8 * b + k - 1)
                    v.tensor_tensor(weighed[:, k % 2, :, :], by_token(d),
                                    top_w[:, c * NJ:(c + 1) * NJ, e:e + 1].to_broadcast([128, NJ, D]), ALU.mult
                                    ).then_inc(drained[d], 1)
                if name in ("stats", "ff_sum"):
                    c = args[0]
                    n = 2 if name == "ff_sum" else args[1]
                    if n == 0:
                        dve.wait_ge(mixed, 8 * b + 4 * (c + 1))
                        src = moe
                    elif n == 1:
                        dve.wait_ge(affine_steps[c], 3 * (b + 1))
                        src = attn
                    else:
                        dve.wait_ge(filled["D"], it.fills("D", stage, ("ff_down", c)))
                        wait(dve, out_done[c], 16 * b)
                        v.scalar_tensor_tensor(out=x2[:, c, :, :].rearrange("p j d -> p (j d)"), in0=bank["D"][:, :],
                                               scalar=INV127, in1=x1[:, c, :, :].rearrange("p j d -> p (j d)"),
                                               op0=ALU.mult, op1=ALU.add).then_inc(drained["D"], 1)
                        dve.wait_ge(drained["D"], it.fills("D", stage, ("ff_down", c)))
                        src = x2
                    for j in range(NJ):
                        ins = v.bn_stats(bst[:, c, j, :], src[:, c, j, :])
                    ins.then_inc(stats_local, 1)
                    dve.wait_ge(stats_local, 1)
                    dve.sem_clear(stats_local)
                    for j in range(NJ):
                        ins = v.bn_aggr(mv[:, c, j, :], bst[:, c, j, :])
                    ins.then_inc(stats_steps[c], 1)
                    dve.wait_ge(stats_steps[c], 6 * b + 2 * n + 1)
                    v.tensor_scalar(ve[:, c, :], mv[:, c, :, 1], EPS, None, ALU.add).then_inc(stats_steps[c], 1)
                if name == "norm":
                    c, n = args
                    src, dst = ((moe, moe), (attn, x1), (x2, x2))[n]
                    dve.wait_ge(rstd_ready[c], 3 * b + n + 1)
                    for j in range(NJ):
                        ins = v.tensor_scalar(dst[:, c, j, :], src[:, c, j, :], mv[:, c, j, 0:1],
                                              rstd[:, c, j:j + 1], ALU.subtract, ALU.mult)
                    ins.then_inc(normed[c], 1)
                if name == "x_low":
                    (c,) = args
                    dve.wait_ge(x_high[c], b + 1)
                    v.tensor_tensor(x1l[:, :], bank["T"][:, :], x1h[:, :].bitcast(F32), ALU.subtract
                                    ).then_inc(drained["T"], 1)
                if name == "ff_mul":
                    (c,) = args
                    for m in range(NH):
                        gate, up = f"U{m % 2}", f"U{(m + NH) % 2}"
                        dve.wait_ge(drained[gate], it.fills(gate, stage, ("ff_up", c), m // 2))
                        dve.wait_ge(filled[up], it.fills(up, stage, ("ff_up", c), (m + NH) // 2))
                        v.scalar_tensor_tensor(out=hh[:, m, :], in0=bank[up][:, :], scalar=INV127, in1=hh[:, m, :],
                                               op0=ALU.mult, op1=ALU.mult).then_inc(drained[up], 1)

            def body(it):
                b = it.b["A"]
                if it.runs["A"]:
                    dve.wait_ge(parts_ready, b + 1)
                    v.tensor_copy(bc_parts[:, :], parts[:, :]).then_inc(bc_parts_ready, 1)
                    v.tensor_tensor(dx[:, :], next_delta[:, :], xT_sb[:, :], ALU.mult).then_inc(dx_ready, 1)
                    clips = dve.value_load(clip_flag[0:1, 0:1], min_val=0, max_val=128)
                    with dve.If(clips > 0):
                        v.tensor_copy(delta[:, :], next_delta[:, :]).then_inc(slow_steps, 1)
                        dve.wait_ge(slow_steps, 1)
                        dve.sem_clear(slow_steps)
                    with dve.Else():
                        dve.nop()
                    dve.nop()
                for s in range(S):
                    if it.runs["A"]:
                        with dve.If(clips > 0):
                            dve.wait_ge(b_ready, S * b + s + 1)
                            dve.wait_ge(dx_ready, b + 1)
                            slow_input(b, s)
                            dve.wait_ge(decay_ready, S * b + s + 1)
                            dve.wait_ge(inp_ready, S * b + s + 1)
                            slow_scan(s)
                        with dve.Else():
                            dve.wait_ge(b_ready, S * b + s + 1)
                            if s == 0:
                                dve.wait_ge(dx_ready, b + 1)
                            fast_input(s)
                            dve.wait_ge(decay_ready, S * b + s + 1)
                            dve.wait_ge(inp_ready, S * b + s + 1)
                            v.tensor_tensor_scan(state[:, :], decay[:, s % NDECAY, :], inp[:, :], 0.0, ALU.mult,
                                                 ALU.add).then_inc(state_ready, 1)
                        dve.nop()
                    for t in it.tasks(DVE_STEPS, 2 * s):
                        run(it, *t)
                    if it.runs["A"]:
                        dve.wait_ge(c_ready, S * b + s + 1)
                        dve.wait_ge(state_ready, S * b + s + 1)
                        wait(dve, added, S * b + s - NPROD + 1)
                        v.tensor_tensor(prod[:, s % NPROD, :], state[:, :], psC[:, :], ALU.mult
                                        ).then_inc(prod_ready, 1)
                    for t in it.tasks(DVE_STEPS, 2 * s + 1):
                        run(it, *t)

            iterate(dve, body)

        @block.gpsimd
        def _(pool):
            g = nc.gpsimd

            def run(it, stage, name, *args):
                b = it.b[stage]
                if name == "bc_rest":
                    pool.wait_ge(parts_high, b + 1)
                    wait(pool, parts_ready, b)
                    g.tensor_tensor(rest[:, :], bcf[:, :], parts[:, :], ALU.subtract
                                    ).then_inc(rest_ready, 1)
                if name == "bound_input":
                    pool.wait_ge(x_scaled, 2 * b + 1)
                    for c in range(2):
                        pool.wait_ge(drained["T"], it.fills("T", "P", ("b_spread", c)))
                        g.tensor_tensor(half(bnd, c), half(bnd, c), half(x_abs, c), ALU.mult).then_inc(bnd_ready, 1)
                if name == "mix":
                    k = args[0]
                    c, e = divmod(k, E)
                    dst = moe[:, c, :, :]
                    (d,) = banks_of(("down", k))
                    pool.wait_ge(drained[d], it.fills(d, "B", ("down", k)))
                    if e == 0:
                        wait(pool, affine_steps[c], 3 * b)
                        pool.wait_ge(drained["T"], it.fills("T", "B", ("y_turn",), 1))
                    wait(pool, mixed, 8 * b + k)
                    g.tensor_tensor(dst, ytok[:, c * NJ:(c + 1) * NJ, 0:D] if e == 0 else dst,
                                    weighed[:, k % 2, :, :], ALU.add
                                    ).then_inc(mixed, 1)
                if name == "rstd":
                    c, n = args
                    pool.wait_ge(stats_steps[c], 6 * b + 2 * n + 2)
                    wait(pool, normed[c], 3 * b + n)
                    g.tensor_tensor(rstd[:, c, :], ve[:, c, :], minus_half[:, :], ALU.pow).then_inc(rstd_ready[c], 1)
                if name == "affine":
                    (c,) = args
                    pool.wait_ge(normed[c], 3 * b + 1)
                    flat = moe[:, c, :, :]
                    lw = lnw_sb[:, :].rearrange("p (o d) -> p o d", o=1).to_broadcast([128, NJ, D])
                    lb = lnb_sb[:, :].rearrange("p (o d) -> p o d", o=1).to_broadcast([128, NJ, D])
                    g.tensor_tensor(flat, flat, lw, ALU.mult).then_inc(affine_steps[c], 1)
                    pool.wait_ge(affine_steps[c], 3 * b + 1)
                    g.tensor_tensor(flat, flat, lb, ALU.add).then_inc(affine_steps[c], 1)
                    pool.wait_ge(affine_steps[c], 3 * b + 2)
                    pool.wait_ge(xt_in[c], 16 * (b + 1))
                    g.tensor_tensor(attn[:, c, :, :], flat, xt[:, c, :, :], ALU.add).then_inc(affine_steps[c], 1)

            def body(it):
                b = it.b["A"]
                for s in range(S):
                    for t in it.tasks(POOL_STEPS, 2 * s):
                        run(it, *t)
                    if it.runs["A"]:
                        pool.wait_ge(prod_ready, S * b + s + 1)
                        if s == 0:
                            pool.wait_ge(x_scaled, 2 * (b + 1))
                        wait(pool, added, S * b + s)
                        if s == S - 1 and it.runs["B"]:
                            pool.wait_ge(filled["U1"], it.fills("U1", "B", ("up", 7), 1))
                        g.tensor_tensor((y if s == S - 1 else yacc)[:, :], prod[:, s % NPROD, :],
                                        (xD if s == 0 else yacc)[:, :], ALU.add).then_inc(added, 1)
                    for t in it.tasks(POOL_STEPS, 2 * s + 1):
                        run(it, *t)

            pool.wait_ge(consts_in, 16 * 16)
            pool.wait_ge(consts_ready, 2)
            iterate(pool, body)


def kernel(**inputs):
    import concourse.bacc as bacc
    from concourse.bass_utils import run_bass_kernel_spmd

    a = {k[3:]: np.asarray(v) for k, v in inputs.items()}
    x = np.ascontiguousarray(a["attn_x"])
    wb, wc = a["attn_WB"], a["attn_WC"]
    none = np.zeros((D, 32), wb.dtype)
    pad = np.zeros(32, wb.dtype)
    bcb = np.concatenate([a["attn_bB"], a["attn_bC"]])
    sel = np.zeros((128, 2 * S), np.float32)
    for row in (0, 64, 96):
        sel[row:row + 2 * S] = np.eye(2 * S, dtype=np.float32)
    arrays = {
        "xT": x.transpose(0, 2, 1), "x": x, "a_log": a["attn_A_log"], "d_param": a["attn_D_param"].reshape(D, 1),
        "wd": a["attn_Wd"], "bd": a["attn_bd"].reshape(D, 1),
        "wbc": np.concatenate([wb, wc, none, wb, wc, wb, wc], axis=1),
        "bbc": np.concatenate([bcb, pad, bcb, bcb]).reshape(128, 1),
        "wr": a["attn_Wr"], "br": a["attn_br"].reshape(1, E), "up_w": a["attn_up_w"],
        "up_b": a["attn_up_b"].reshape(E * NF, 128).T, "down_w": a["attn_down_w"],
        "down_b": a["attn_down_b"].reshape(1, E * D), "ln_w": a["attn_ln_w"].reshape(1, D),
        "ln_b": a["attn_ln_b"].reshape(1, D), "wg": a["ffn_w_gate"].T, "wu": a["ffn_w_up"].T,
        "wdn": a["ffn_w_down"].T, "ident": np.eye(128, dtype=np.float32), "sel": sel,
        "rev": np.arange(E, 0, -1, dtype=np.float32).reshape(1, E),
    }
    nc = bacc.Bacc("TRN2", target_bir_lowering=False, num_devices=1)
    feed, args = {}, []
    for name, v in arrays.items():
        v = np.ascontiguousarray(v)
        feed[f"in_{name}"] = v
        args.append(nc.dram_tensor(f"in_{name}", v.shape, mybir.dt.from_np(v.dtype), kind="ExternalInput").ap())
    out = nc.dram_tensor("out", (NB, L, D), F32, kind="ExternalOutput").ap()
    ssm_moe_ffn_kernel(nc, *args, out)
    r = run_bass_kernel_spmd(nc, [feed], core_ids=[0])
    return r.results[0]["out"]
```
